# Optimizing a Trainium2 kernel written in Bass

```python
import numpy as np
import jax
import jax.numpy as jnp

def _softmax(x, axis=-1):
    return jax.nn.softmax(x, axis=axis)

def _gelu(x):
    return jax.nn.gelu(x, approximate=True)

def _silu(x):
    return jax.nn.silu(x)

def _sigmoid(x):
    return jax.nn.sigmoid(x)

def _layernorm(x, axis=-1, eps=1e-05):
    m = jnp.mean(x, axis=axis, keepdims=True)
    v = jnp.var(x, axis=axis, keepdims=True)
    return (x - m) / jnp.sqrt(v + eps)

def _scatter_add(tgt, idx, src, axis=0):
    return tgt.at[idx].add(src)

def _segment_sum(src, seg, n):
    return jax.ops.segment_sum(src, seg, n)
kernel_name = 'mk_decoder_postln_d2_seqx_r8_67c031'

def setup_inputs(seed: int=0):
    np.random.seed(seed)
    _w = jnp.asarray

    def _rec_inputs():
        import jax
        import jax.numpy as jnp
        _rk = jax.random.key(seed)
        x = -0.0003929 + 0.9999 * jax.random.normal(jax.random.fold_in(_rk, 1), (16, 128, 128), jnp.float32)
        _lenS = 128 - jax.random.randint(jax.random.fold_in(_rk, 7), (16,), 0, max(1, 128 // 4) + 1, jnp.int32)
        _lenS2 = 128 - jax.random.randint(jax.random.fold_in(_rk, 8), (16,), 0, max(1, 128 // 4) + 1, jnp.int32)
        _ctx_768P = jax.random.normal(jax.random.fold_in(_rk, 11), (16, 16, 96), jnp.float32)
        _ctx_768c = jax.random.dirichlet(jax.random.fold_in(_rk, 511), 0.3 * jnp.ones((16,), jnp.float32), (16, 128))
        _ctx_768t = jnp.einsum('bsk,bkd->bsd', _ctx_768c, _ctx_768P)
        _ctx_768t = _ctx_768t * jax.lax.rsqrt(jnp.mean(jnp.square(_ctx_768t)) + 1e-12) * 0.953939
        ctx_768 = -7.36909e-05 + 0.999899 * (_ctx_768t + 0.3 * jax.random.normal(jax.random.fold_in(_rk, 611), (16, 128, 96), jnp.float32))
        return (x, ctx_768)
    x, ctx_768 = _rec_inputs()

    def _L0_attn_setup():
        import jax, jax.numpy as jnp
        import numpy as np
        B, T, C, H = (4, 256, 128, 16)
        D = C // H
        key = jax.random.key(seed)
        ks = jax.random.split(key, 5)
        scale = 0.02
        return {'x': jax.random.normal(ks[0], (B, T, C), dtype=jnp.float32), 'w_qkv': jax.random.normal(ks[1], (C, 3 * C), dtype=jnp.float32) * scale, 'b_qkv': jnp.zeros((3 * C,), dtype=jnp.float32), 'w_out': jax.random.normal(ks[2], (C, C), dtype=jnp.float32) * scale, 'b_out': jnp.zeros((C,), dtype=jnp.float32)}
    _L0_attn_all = _L0_attn_setup()
    _L0_attn_in = {k: v for k, v in _L0_attn_all.items() if k in ('w_qkv', 'b_qkv', 'w_out', 'b_out')}
    del _L0_attn_all

    def _L0_xattn_setup():
        import jax, jax.numpy as jnp
        import numpy as np
        EPS = 1e-08
        key = jax.random.key(seed)
        kv, kt, k1, k2, k3, k4 = jax.random.split(key, 6)
        B, S = (16, 128)
        VD, TD, H = (128, 96, 64)
        visual_features = jax.random.normal(kv, (B, S, VD), dtype=jnp.float32)
        text_features = jax.random.normal(kt, (B, S, TD), dtype=jnp.float32)
        Wv = jax.random.normal(k1, (H, VD), dtype=jnp.float32) * (1.0 / np.sqrt(VD))
        bv = jax.random.normal(k2, (H,), dtype=jnp.float32) * 0.01
        Wt = jax.random.normal(k3, (H, TD), dtype=jnp.float32) * (1.0 / np.sqrt(TD))
        bt = jax.random.normal(k4, (H,), dtype=jnp.float32) * 0.01
        return {'visual_features': visual_features, 'text_features': text_features, 'Wv': Wv, 'bv': bv, 'Wt': Wt, 'bt': bt}
    _L0_xattn_all = _L0_xattn_setup()
    _L0_xattn_in = {k: v for k, v in _L0_xattn_all.items() if k in ('Wv', 'bv', 'Wt', 'bt')}
    del _L0_xattn_all

    def _L0_ffn_setup():
        import jax, jax.numpy as jnp
        import numpy as np
        D = 128
        E = 8
        H = 256
        TOP_K = 2
        ALPHA = 0.5
        LN_EPS = 1e-05

        def _experts_all(x, W1, b1, W2, b2):
            h = jax.nn.relu(jnp.einsum('bld,edh->eblh', x, W1) + b1[:, None, None, :])
            return jnp.einsum('eblh,ehd->ebld', h, W2) + b2[:, None, None, :]

        def _selected_expert(x, expert_idx, W1, b1, W2, b2):
            oh = jax.nn.one_hot(expert_idx, E, dtype=x.dtype)
            return jnp.einsum('ebld,ble->bld', _experts_all(x, W1, b1, W2, b2), oh)

        def _layer_norm(x, gamma, beta):
            mu = jnp.mean(x, axis=-1, keepdims=True)
            var = jnp.mean(jnp.square(x - mu), axis=-1, keepdims=True)
            return (x - mu) * jax.lax.rsqrt(var + LN_EPS) * gamma + beta
        key = jax.random.key(seed)
        ks = jax.random.split(key, 8)
        x = jax.random.normal(ks[0], (2, 256, D), dtype=jnp.float32)
        gate_W = jax.random.normal(ks[1], (D, E), dtype=jnp.float32) * 0.02
        gate_b = jnp.zeros((E,), dtype=jnp.float32)
        W1 = jax.random.normal(ks[2], (E, D, H), dtype=jnp.float32) * 0.02
        b1 = jnp.zeros((E, H), dtype=jnp.float32)
        W2 = jax.random.normal(ks[3], (E, H, D), dtype=jnp.float32) * 0.02
        b2 = jnp.zeros((E, D), dtype=jnp.float32)
        ln_gamma = jnp.ones((D,), dtype=jnp.float32)
        ln_beta = jnp.zeros((D,), dtype=jnp.float32)
        return {'x': x, 'gate_W': gate_W, 'gate_b': gate_b, 'W1': W1, 'b1': b1, 'W2': W2, 'b2': b2, 'ln_gamma': ln_gamma, 'ln_beta': ln_beta}
    _L0_ffn_all = _L0_ffn_setup()
    _L0_ffn_in = {k: v for k, v in _L0_ffn_all.items() if k in ('gate_W', 'gate_b', 'W1', 'b1', 'W2', 'b2', 'ln_gamma', 'ln_beta')}
    del _L0_ffn_all

    def _L1_attn_setup():
        import jax, jax.numpy as jnp
        import numpy as np
        D_MODEL = 128
        NUM_HEADS = 16
        HEAD_DIM = D_MODEL // NUM_HEADS
        WINDOW = 128
        NEG_INF = -1e+30

        def _sliding_mask(seqlen: int) -> jnp.ndarray:
            rel = jnp.arange(seqlen)[:, None] - jnp.arange(seqlen)[None, :]
            allowed = (rel >= 0) & (rel < WINDOW)
            return jnp.where(allowed, 0.0, NEG_INF).astype(jnp.float32)
        key = jax.random.key(seed)
        kx, kq, kk, kv, ko = jax.random.split(key, 5)
        B, S = (2, 256)
        scale = 0.02
        x = jax.random.normal(kx, (B, S, D_MODEL), dtype=jnp.float32)
        Wq = jax.random.normal(kq, (D_MODEL, D_MODEL), dtype=jnp.float32) * scale
        Wk = jax.random.normal(kk, (D_MODEL, D_MODEL), dtype=jnp.float32) * scale
        Wv = jax.random.normal(kv, (D_MODEL, D_MODEL), dtype=jnp.float32) * scale
        Wo = jax.random.normal(ko, (D_MODEL, D_MODEL), dtype=jnp.float32) * scale
        return {'x': x, 'Wq': Wq, 'Wk': Wk, 'Wv': Wv, 'Wo': Wo}
    _L1_attn_all = _L1_attn_setup()
    _L1_attn_in = {k: v for k, v in _L1_attn_all.items() if k in ('Wq', 'Wk', 'Wv', 'Wo')}
    del _L1_attn_all

    def _L1_xattn_setup():
        import jax, jax.numpy as jnp
        import numpy as np
        N_HEADS = 16
        DIM_EMBED = 128
        DIM_CROSS = 96
        DIM_HEAD = DIM_EMBED // N_HEADS
        key = jax.random.key(seed)
        ks = jax.random.split(key, 10)
        B, Sq, Sk = (8, 512, 77)
        s_e = 1.0 / np.sqrt(DIM_EMBED)
        s_c = 1.0 / np.sqrt(DIM_CROSS)
        return {'x': jax.random.normal(ks[0], (B, Sq, DIM_EMBED), jnp.float32), 'y': jax.random.normal(ks[1], (B, Sk, DIM_CROSS), jnp.float32), 'wq': jax.random.normal(ks[2], (DIM_EMBED, DIM_EMBED), jnp.float32) * s_e, 'bq': jax.random.normal(ks[3], (DIM_EMBED,), jnp.float32) * 0.01, 'wk': jax.random.normal(ks[4], (DIM_CROSS, DIM_EMBED), jnp.float32) * s_c, 'bk': jax.random.normal(ks[5], (DIM_EMBED,), jnp.float32) * 0.01, 'wv': jax.random.normal(ks[6], (DIM_CROSS, DIM_EMBED), jnp.float32) * s_c, 'bv': jax.random.normal(ks[7], (DIM_EMBED,), jnp.float32) * 0.01, 'wo': jax.random.normal(ks[8], (DIM_EMBED, DIM_EMBED), jnp.float32) * s_e, 'bo': jax.random.normal(ks[9], (DIM_EMBED,), jnp.float32) * 0.01}
    _L1_xattn_all = _L1_xattn_setup()
    _L1_xattn_in = {k: v for k, v in _L1_xattn_all.items() if k in ('wq', 'bq', 'wk', 'bk', 'wv', 'bv', 'wo', 'bo')}
    del _L1_xattn_all

    def _L1_ffn_setup():
        import jax, jax.numpy as jnp
        import numpy as np
        N_EXPERTS = 16
        TOP_K = int(N_EXPERTS * 0.2)
        EPS = 1e-12
        key = jax.random.key(seed)
        ks = jax.random.split(key, 6)
        B, T, D, H, E = (4, 128, 128, 256, N_EXPERTS)
        x = jax.random.normal(ks[0], (B, T, D), dtype=jnp.float32)
        gate = jax.random.normal(ks[1], (D, E), dtype=jnp.float32)
        W1 = jax.random.normal(ks[2], (E, D, H), dtype=jnp.float32) * (1.0 / np.sqrt(D))
        b1 = jax.random.normal(ks[3], (E, H), dtype=jnp.float32) * 0.02
        W2 = jax.random.normal(ks[4], (E, H, D), dtype=jnp.float32) * (1.0 / np.sqrt(H))
        b2 = jax.random.normal(ks[5], (E, D), dtype=jnp.float32) * 0.02
        return {'x': x, 'gate': gate, 'W1': W1, 'b1': b1, 'W2': W2, 'b2': b2}
    _L1_ffn_all = _L1_ffn_setup()
    _L1_ffn_in = {k: v for k, v in _L1_ffn_all.items() if k in ('gate', 'W1', 'b1', 'W2', 'b2')}
    del _L1_ffn_all
    return {'x': x, 'ctx_768': ctx_768, 'L0_attn_w_qkv': _L0_attn_in['w_qkv'], 'L0_attn_b_qkv': _L0_attn_in['b_qkv'], 'L0_attn_w_out': _L0_attn_in['w_out'], 'L0_attn_b_out': _L0_attn_in['b_out'], 'L0_xattn_Wv': _L0_xattn_in['Wv'], 'L0_xattn_bv': _L0_xattn_in['bv'], 'L0_xattn_Wt': _L0_xattn_in['Wt'], 'L0_xattn_bt': _L0_xattn_in['bt'], 'L0_ffn_gate_W': _L0_ffn_in['gate_W'], 'L0_ffn_gate_b': _L0_ffn_in['gate_b'], 'L0_ffn_W1': _L0_ffn_in['W1'], 'L0_ffn_b1': _L0_ffn_in['b1'], 'L0_ffn_W2': _L0_ffn_in['W2'], 'L0_ffn_b2': _L0_ffn_in['b2'], 'L0_ffn_ln_gamma': _L0_ffn_in['ln_gamma'], 'L0_ffn_ln_beta': _L0_ffn_in['ln_beta'], 'L1_attn_Wq': _L1_attn_in['Wq'], 'L1_attn_Wk': _L1_attn_in['Wk'], 'L1_attn_Wv': _L1_attn_in['Wv'], 'L1_attn_Wo': _L1_attn_in['Wo'], 'L1_xattn_wq': _L1_xattn_in['wq'], 'L1_xattn_bq': _L1_xattn_in['bq'], 'L1_xattn_wk': _L1_xattn_in['wk'], 'L1_xattn_bk': _L1_xattn_in['bk'], 'L1_xattn_wv': _L1_xattn_in['wv'], 'L1_xattn_bv': _L1_xattn_in['bv'], 'L1_xattn_wo': _L1_xattn_in['wo'], 'L1_xattn_bo': _L1_xattn_in['bo'], 'L1_ffn_gate': _L1_ffn_in['gate'], 'L1_ffn_W1': _L1_ffn_in['W1'], 'L1_ffn_b1': _L1_ffn_in['b1'], 'L1_ffn_W2': _L1_ffn_in['W2'], 'L1_ffn_b2': _L1_ffn_in['b2']}

def reference(x, ctx_768, L0_attn_w_qkv, L0_attn_b_qkv, L0_attn_w_out, L0_attn_b_out, L0_xattn_Wv, L0_xattn_bv, L0_xattn_Wt, L0_xattn_bt, L0_ffn_gate_W, L0_ffn_gate_b, L0_ffn_W1, L0_ffn_b1, L0_ffn_W2, L0_ffn_b2, L0_ffn_ln_gamma, L0_ffn_ln_beta, L1_attn_Wq, L1_attn_Wk, L1_attn_Wv, L1_attn_Wo, L1_xattn_wq, L1_xattn_bq, L1_xattn_wk, L1_xattn_bk, L1_xattn_wv, L1_xattn_bv, L1_xattn_wo, L1_xattn_bo, L1_ffn_gate, L1_ffn_W1, L1_ffn_b1, L1_ffn_W2, L1_ffn_b2):
    import jax
    import jax.numpy as jnp

    def _L0_attn_ref(x, w_qkv, b_qkv, w_out, b_out):
        import jax, jax.numpy as jnp
        import numpy as np
        B, T, C, H = (4, 256, 128, 16)
        D = C // H
        Bx, Tx, Cx = x.shape
        qkv = x @ w_qkv + b_qkv
        q, k, v = jnp.split(qkv, 3, axis=-1)

        def heads(t):
            return t.reshape(Bx, Tx, H, D).transpose(0, 2, 1, 3)
        q, k, v = (heads(q), heads(k), heads(v))
        scores = jnp.einsum('bhtd,bhsd->bhts', q, k) / jnp.sqrt(jnp.float32(D))
        causal = jnp.tril(jnp.ones((Tx, Tx), dtype=bool))
        scores = jnp.where(causal[None, None], scores, -jnp.inf)
        attn = jax.nn.softmax(scores, axis=-1)
        y = jnp.einsum('bhts,bhsd->bhtd', attn, v)
        y = y.transpose(0, 2, 1, 3).reshape(Bx, Tx, Cx)
        return y @ w_out + b_out

    def _L0_xattn_ref(visual_features, text_features, Wv, bv, Wt, bt):
        import jax, jax.numpy as jnp
        import numpy as np
        EPS = 1e-08
        v = jnp.einsum('bsd,hd->bsh', visual_features, Wv) + bv
        t = jnp.einsum('bsd,hd->bsh', text_features, Wt) + bt
        dots = jnp.einsum('bih,bjh->bij', v, t)
        vn = jnp.linalg.norm(v, axis=-1)
        tn = jnp.linalg.norm(t, axis=-1)
        denom = jnp.maximum(vn[:, :, None] * tn[:, None, :], EPS)
        return dots / denom

    def _L0_ffn_ref(x, gate_W, gate_b, W1, b1, W2, b2, ln_gamma, ln_beta):
        import jax, jax.numpy as jnp
        import numpy as np
        D = 128
        E = 8
        H = 256
        TOP_K = 2
        ALPHA = 0.5
        LN_EPS = 1e-05

        def _experts_all(x, W1, b1, W2, b2):
            h = jax.nn.relu(jnp.einsum('bld,edh->eblh', x, W1) + b1[:, None, None, :])
            return jnp.einsum('eblh,ehd->ebld', h, W2) + b2[:, None, None, :]

        def _selected_expert(x, expert_idx, W1, b1, W2, b2):
            oh = jax.nn.one_hot(expert_idx, E, dtype=x.dtype)
            return jnp.einsum('ebld,ble->bld', _experts_all(x, W1, b1, W2, b2), oh)

        def _layer_norm(x, gamma, beta):
            mu = jnp.mean(x, axis=-1, keepdims=True)
            var = jnp.mean(jnp.square(x - mu), axis=-1, keepdims=True)
            return (x - mu) * jax.lax.rsqrt(var + LN_EPS) * gamma + beta
        residual = x
        gate_logits = jnp.einsum('bld,de->ble', x, gate_W) + gate_b
        gate_weights = jax.nn.softmax(gate_logits, axis=-1)
        topk_vals, topk_idx = jax.lax.top_k(gate_weights, TOP_K)
        boost = jax.lax.stop_gradient(x)
        outs = []
        for i in range(TOP_K):
            eo = _selected_expert(boost, topk_idx[:, :, i], W1, b1, W2, b2)
            outs.append(eo)
            if i < TOP_K - 1:
                boost = boost + ALPHA * jax.lax.stop_gradient(eo)
        fused = sum((topk_vals[:, :, i:i + 1] * outs[i] for i in range(TOP_K)))
        return _layer_norm(residual + fused, ln_gamma, ln_beta)

    def _L1_attn_ref(x, Wq, Wk, Wv, Wo):
        import jax, jax.numpy as jnp
        import numpy as np
        D_MODEL = 128
        NUM_HEADS = 16
        HEAD_DIM = D_MODEL // NUM_HEADS
        WINDOW = 128
        NEG_INF = -1e+30

        def _sliding_mask(seqlen: int) -> jnp.ndarray:
            rel = jnp.arange(seqlen)[:, None] - jnp.arange(seqlen)[None, :]
            allowed = (rel >= 0) & (rel < WINDOW)
            return jnp.where(allowed, 0.0, NEG_INF).astype(jnp.float32)
        B, S, _ = x.shape

        def proj(W):
            y = jnp.einsum('bsd,ed->bse', x, W)
            return y.reshape(B, S, NUM_HEADS, HEAD_DIM).transpose(0, 2, 1, 3)
        q, k, v = (proj(Wq), proj(Wk), proj(Wv))
        scale = 1.0 / jnp.sqrt(jnp.float32(HEAD_DIM))
        scores = jnp.einsum('bhqd,bhkd->bhqk', q, k) * scale + _sliding_mask(S)
        attn = jax.nn.softmax(scores, axis=-1)
        y = jnp.einsum('bhqk,bhkd->bhqd', attn, v)
        y = y.transpose(0, 2, 1, 3).reshape(B, S, D_MODEL)
        return jnp.einsum('bsd,ed->bse', y, Wo)

    def _L1_xattn_ref(x, y, wq, bq, wk, bk, wv, bv, wo, bo):
        import jax, jax.numpy as jnp
        import numpy as np
        N_HEADS = 16
        DIM_EMBED = 128
        DIM_CROSS = 96
        DIM_HEAD = DIM_EMBED // N_HEADS
        B, Sq, E = x.shape
        H, D = (N_HEADS, DIM_HEAD)
        q = (x @ wq + bq).reshape(B, Sq, H, D).transpose(0, 2, 1, 3)
        k = (y @ wk + bk).reshape(B, -1, H, D).transpose(0, 2, 1, 3)
        v = (y @ wv + bv).reshape(B, -1, H, D).transpose(0, 2, 1, 3)
        scores = jnp.einsum('bhqd,bhkd->bhqk', q, k) / jnp.sqrt(jnp.asarray(D, x.dtype))
        attn = jax.nn.softmax(scores, axis=-1)
        out = jnp.einsum('bhqk,bhkd->bhqd', attn, v)
        out = out.transpose(0, 2, 1, 3).reshape(B, Sq, E)
        return out @ wo + bo

    def _L1_ffn_ref(x, gate, W1, b1, W2, b2):
        import jax, jax.numpy as jnp
        import numpy as np
        N_EXPERTS = 16
        TOP_K = int(N_EXPERTS * 0.2)
        EPS = 1e-12
        raw_gate = jax.nn.softmax(jnp.einsum('btd,de->bte', x, gate), axis=-1)
        _, topk_idx = jax.lax.top_k(raw_gate, TOP_K)
        mask = jax.nn.one_hot(topk_idx, raw_gate.shape[-1], dtype=raw_gate.dtype).sum(axis=2)
        gate_topk = mask * raw_gate
        gate_topk = gate_topk / jnp.maximum(jnp.sum(jnp.abs(gate_topk), axis=-1, keepdims=True), EPS)
        hidden = jax.nn.relu(jnp.einsum('btd,edh->bteh', x, W1) + b1)
        expert_out = jnp.einsum('bteh,ehd->bted', hidden, W2) + b2
        return jnp.einsum('bte,bted->btd', gate_topk, expert_out)
    x = _layernorm(x + _L0_attn_ref(x, L0_attn_w_qkv, L0_attn_b_qkv, L0_attn_w_out, L0_attn_b_out), axis=-1)
    x = _layernorm(x + _L0_xattn_ref(x, ctx_768, L0_xattn_Wv, L0_xattn_bv, L0_xattn_Wt, L0_xattn_bt), axis=-1)
    x = _layernorm(x + _L0_ffn_ref(x, L0_ffn_gate_W, L0_ffn_gate_b, L0_ffn_W1, L0_ffn_b1, L0_ffn_W2, L0_ffn_b2, L0_ffn_ln_gamma, L0_ffn_ln_beta), axis=-1)
    x = _layernorm(x + _L1_attn_ref(x, L1_attn_Wq, L1_attn_Wk, L1_attn_Wv, L1_attn_Wo), axis=-1)
    x = _layernorm(x + _L1_xattn_ref(x, ctx_768, L1_xattn_wq, L1_xattn_bq, L1_xattn_wk, L1_xattn_bk, L1_xattn_wv, L1_xattn_bv, L1_xattn_wo, L1_xattn_bo), axis=-1)
    x = _layernorm(x + _L1_ffn_ref(x, L1_ffn_gate, L1_ffn_W1, L1_ffn_b1, L1_ffn_W2, L1_ffn_b2), axis=-1)
    return x

_drawn_inputs = setup_inputs


def setup_inputs(seed=0):
    import zlib

    import numpy as np

    out = dict(_drawn_inputs(seed))
    spreads = {'L0_attn_b_qkv': (0.0, 0.1),
     'L0_attn_b_out': (0.0, 0.1),
     'L0_ffn_gate_b': (0.0, 0.56),
     'L0_ffn_b1': (0.0, 0.8),
     'L0_ffn_b2': (0.0, 0.475),
     'L0_ffn_ln_gamma': (1.0, 0.2),
     'L0_ffn_ln_beta': (0.0, 0.1)}
    factors = {'L0_attn_w_qkv': 3.639,
     'L0_xattn_bv': 8.0,
     'L0_xattn_bt': 21.914,
     'L0_ffn_gate_W': 3.181,
     'L0_ffn_W1': 6.447,
     'L0_ffn_W2': 4.93,
     'L1_attn_Wq': 8.0,
     'L1_attn_Wk': 8.0,
     'L1_attn_Wv': 3.23,
     'L1_attn_Wo': 3.271,
     'L1_xattn_bq': 8.0,
     'L1_xattn_bk': 64.0,
     'L1_xattn_bv': 3.275,
     'L1_xattn_bo': 3.547,
     'L1_ffn_b1': 5.127,
     'L1_ffn_b2': 3.524}
    for name, (base, spread) in spreads.items():
        noise = np.random.default_rng([zlib.crc32(name.encode()), seed]).standard_normal(out[name].shape)
        drawn = base * np.exp(spread * noise) if base else spread * noise
        out[name] = jnp.asarray(drawn.astype(out[name].dtype))
    for name, factor in factors.items():
        out[name] = (out[name] * factor).astype(out[name].dtype)
    return out
```

```python
import numpy as np
import concourse.bass as bass
from concourse import mybir
from contextlib import ExitStack

B, T, C, H = 16, 128, 128, 16
D = C // H
CTX = 96
XH = 64
FH = 256
E0, E1 = 8, 16
GB = 4
NG = B // GB
HU = 4
UN = H // HU
LN_EPS = 1e-5
COS_EPS = 1e-8
NORM_FLOOR = 1e-30
BIG = 1e30

F32 = mybir.dt.float32
BF16 = mybir.dt.bfloat16
ALU = mybir.AluOpType
ACT = mybir.ActivationFunctionType
AX = mybir.AxisListType.X


def need(eng, sem, value):
    if isinstance(value, int) and value <= 0:
        return
    eng.wait_ge(sem, value)


def real(b, n):
    return not isinstance(b, int) or 0 <= b < n


def decoder(nc, a, out):
    ctx = ExitStack()
    with ctx:
        def sb(name, shape, dt=F32):
            return ctx.enter_context(nc.sbuf_tensor(name, shape, dt))

        def sem(name):
            return ctx.enter_context(nc.semaphore(name))

        bank = [ctx.enter_context(nc.psum_tensor(f"bank{n}", [128, 512], F32)) for n in range(8)]

        x_all = sb("x_all", [128, B * C])
        ctx_all = sb("ctx_all", [128, B * CTX])
        ident = sb("ident", [128, 128])
        ident_b = sb("ident_b", [128, 128], BF16)
        causal = sb("causal", [128, 128])
        causal_b = sb("causal_b", [128, HU, 128], BF16)
        sel = sb("sel", [128, 2, UN])
        sel_q = sb("sel_q", [128, UN, 128])
        sel_k = sb("sel_k", [128, HU, 128])
        ones = sb("ones", [128, 128])
        minus_half = sb("minus_half", [128, 2 * GB])
        ln_eps = sb("ln_eps", [128, GB])
        zero_col = sb("zero_col", [128, 1])
        zero_row = sb("zero_row", [128, 128])

        w_qkv = sb("w_qkv", [128, 3 * C])
        bq0 = sb("bq0", [128, 1])
        bk0 = sb("bk0", [128, 1])
        bv0 = sb("bv0", [128, C])
        w_out0 = sb("w_out0", [128, C])
        bo0 = sb("bo0", [128, C])

        raw = sb("raw", [128, 8, 128])
        wT = sb("wT", [128, 8, 128])
        b1_0 = wT[:, 6, 0:2 * E0]
        b1_1 = wT[:, 7, 0:2 * E1]
        bvx = sb("bvx", [XH, 1])
        btx = sb("btx", [XH, 1])

        wqx = sb("wqx", [128, C])
        wkx = sb("wkx", [CTX, C])
        wvx = sb("wvx", [CTX, C])
        wox = sb("wox", [128, C])
        bq1 = sb("bq1", [128, 1])
        bk1 = sb("bk1", [128, 1])
        bv1 = sb("bv1", [128, C])
        bo1 = sb("bo1", [128, C])

        gate_w0 = sb("gate_w0", [128, E0])
        gate_b0 = sb("gate_b0", [128, E0])
        gate_w1 = sb("gate_w1", [128, E1])
        gamma = sb("gamma", [128, C])
        beta = sb("beta", [128, C])
        w1_0 = sb("w1_0", [128, E0, FH])
        w2_0 = sb("w2_0", [128, E0, 2, C])
        w1_1 = sb("w1_1", [128, E1, FH])
        w2_1 = sb("w2_1", [128, E1, 2, C])
        b2_0 = sb("b2_0", [128, C])
        b2_1 = sb("b2_1", [128, C])
        rank0 = sb("rank0", [128, E0])
        rank1 = sb("rank1", [128, E1])

        xs = sb("xs", [128, 2, C])
        cs = sb("cs", [128, 2, CTX])
        xT = sb("xT", [128, 2, 128])
        cT = sb("cT", [CTX, 2, 128])
        qg = sb("qg", [128, 2, UN, 128])
        kj = sb("kj", [128, 2, HU, 128])
        HALF = 8 * 136
        v_pad = sb("v_pad", [128, 2, 2 * HALF])
        mx = sb("mx", [128, UN, HU])
        shifted = sb("shifted", [128, 2, HU, 128])
        probs = sb("probs", [128, 4, HU, 128])
        probsT = sb("probsT", [128, 2, HU, 128])
        rden = sb("rden", [128, 2, 128])
        oT = sb("oT", [128, 2, 128])
        xb = sb("xb", [128, 2, C])
        y = sb("y", [128, 2, C])
        st = sb("st", [128, 2, 6])
        mv = sb("mv", [128, 2, 2])
        ve = sb("ve", [128, 2, 1])
        rs = sb("rs", [128, 2, 1])

        xg = sb("xg", [128, GB, C])
        cg = sb("cg", [128, GB, CTX])
        xgT = sb("xgT", [128, GB * 128])
        cgT = sb("cgT", [CTX, GB * 128])
        vT = sb("vT", [XH, GB * 128])
        vT2 = sb("vT2", [XH, GB * 128])
        tT = sb("tT", [XH, GB * 128])
        tT2 = sb("tT2", [XH, GB * 128])
        nrm = sb("nrm", [128, 2 * GB])
        rn = sb("rn", [128, 2 * GB])
        diag = sb("diag", [128, GB, 128])
        cosw = sb("cosw", [128, GB, 128])
        yg = sb("yg", [128, GB, C])
        boostT = sb("boostT", [128, GB * 128])
        hid = sb("hid", [128, 2, 2, GB * 128])
        acc = sb("acc", [128, GB, C])
        eo1 = sb("eo1", [128, GB, C])
        cpad = sb("cpad", [128, GB, 128])
        cpT = sb("cpT", [128, GB, 128])
        lg = sb("lg", [128, GB, E1])
        pr = sb("pr", [128, GB, E1])
        left = sb("left", [128, GB, E1])
        hot = sb("hot", [128, GB, E1])
        coef1 = sb("coef1", [128, GB, E1])
        coef2 = sb("coef2", [128, GB, E1])
        sm = sb("sm", [128, GB])
        sm2 = sb("sm2", [128, GB])
        g1 = sb("g1", [128, GB])
        gst = sb("gst", [128, GB, 6])
        gmv = sb("gmv", [128, GB, 2])
        gve = sb("gve", [128, GB])
        grs = sb("grs", [128, GB])
        xo = sb("xo", [128, GB, C])

        s_in = sem("s_in")
        s_w = sem("s_w")
        s_const = sem("s_const")
        s_zeroed = sem("s_zeroed")
        s_b2 = sem("s_b2")
        s_rawT = sem("s_rawT")
        s_wT = sem("s_wT")

        small_in = [(ident[:], a["ident"]), (causal[:], a["causal"]), (sel[:], a["sel"]),
                    (x_all[:].rearrange("p (b c) -> p b c", b=B), a["x"].rearrange("b p c -> p b c")),
                    (w_qkv[:], a["L0_attn_w_qkv"]),
                    (bq0[:], a["L0_attn_b_qkv"][0:C].rearrange("(c o) -> c o", o=1)),
                    (bk0[:], a["L0_attn_b_qkv"][C:2 * C].rearrange("(c o) -> c o", o=1)),
                    (bv0[:], a["L0_attn_b_qkv"][2 * C:3 * C].partition_broadcast(128)),
                    (w_out0[:], a["L0_attn_w_out"]),
                    (bo0[:], a["L0_attn_b_out"].partition_broadcast(128)),
                    (raw[0:XH, 0, :], a["L0_xattn_Wv"]), (raw[0:XH, 1, 0:CTX], a["L0_xattn_Wt"]),
                    (raw[:, 2, :], a["L1_attn_Wq"]), (raw[:, 3, :], a["L1_attn_Wk"]),
                    (raw[:, 4, :], a["L1_attn_Wv"]), (raw[:, 5, :], a["L1_attn_Wo"]),
                    (raw[0:2 * E0, 6, :], a["L0_ffn_b1"].rearrange("e (k h) -> (e k) h", k=2)),
                    (raw[0:2 * E1, 7, :], a["L1_ffn_b1"].rearrange("e (k h) -> (e k) h", k=2))]
        TURNED = ((XH, C), (XH, CTX), (C, C), (C, C), (C, C), (C, C), (2 * E0, 128), (2 * E1, 128))
        late_in = [(ctx_all[:].rearrange("p (b c) -> p b c", b=B), a["ctx_768"].rearrange("b p c -> p b c")),
                   (bvx[:], a["L0_xattn_bv"].rearrange("(c o) -> c o", o=1)),
                   (btx[:], a["L0_xattn_bt"].rearrange("(c o) -> c o", o=1)),
                   (gate_w0[:], a["L0_ffn_gate_W"]), (gate_b0[:], a["L0_ffn_gate_b"].partition_broadcast(128)),
                   (rank0[:], a["rank0"].partition_broadcast(128)),
                   (w1_0[:], a["L0_ffn_W1"].rearrange("e c h -> c e h")),
                   (w2_0[:], a["L0_ffn_W2"].rearrange("e (k h) c -> h e k c", k=2)),
                   (gamma[:], a["L0_ffn_ln_gamma"].partition_broadcast(128)),
                   (beta[:], a["L0_ffn_ln_beta"].partition_broadcast(128)),
                   (wqx[:], a["L1_xattn_wq"]), (wkx[:], a["L1_xattn_wk"]),
                   (wvx[:], a["L1_xattn_wv"]), (wox[:], a["L1_xattn_wo"]),
                   (bq1[:], a["L1_xattn_bq"].rearrange("(c o) -> c o", o=1)),
                   (bk1[:], a["L1_xattn_bk"].rearrange("(c o) -> c o", o=1)),
                   (bv1[:], a["L1_xattn_bv"].partition_broadcast(128)),
                   (bo1[:], a["L1_xattn_bo"].partition_broadcast(128)),
                   (gate_w1[:], a["L1_ffn_gate"]), (rank1[:], a["rank1"].partition_broadcast(128)),
                   (w1_1[:], a["L1_ffn_W1"].rearrange("e c h -> c e h")),
                   (w2_1[:], a["L1_ffn_W2"].rearrange("e (k h) c -> h e k c", k=2))]
        padded_in = [(b2_0[0:E0, :], a["L0_ffn_b2"]), (b2_1[0:E1, :], a["L1_ffn_b2"])]
        LATE = 16 * len(late_in)
        CONSTS = 12

        class Attention:

            def __init__(self, name, wq, wk, wv, wo, bq, bk, bv, bo, masked, cross, before):
                self.wq, self.wk, self.wv, self.wo, self.bq = wq, wk, wv, wo, bq
                self.bk, self.bv, self.bo, self.masked, self.cross = bk, bv, bo, masked, cross
                self.before = before
                self.copied = sem(name + "_copied")
                self.turned = sem(name + "_turned")
                self.xT = sem(name + "_xT")
                self.qkv = sem(name + "_qkv")
                self.q = sem(name + "_q")
                self.k = sem(name + "_k")
                self.v = sem(name + "_v")
                self.scores = sem(name + "_scores")
                self.max = sem(name + "_max")
                self.shifted = sem(name + "_shifted")
                self.exp = sem(name + "_exp")
                self.pT = sem(name + "_pT")
                self.probsT = sem(name + "_probsT")
                self.pv = sem(name + "_pv")
                self.rden = sem(name + "_rden")
                self.oT = sem(name + "_oT")
                self.proj = sem(name + "_proj")
                self.res = sem(name + "_res")
                self.y = sem(name + "_y")
                self.mv = sem(name + "_mv")
                self.ve = sem(name + "_ve")
                self.rstd = sem(name + "_rstd")
                self.x = sem(name + "_x")

        class Experts:

            def __init__(self, name, n, rounds, gw, gb, w1, w2, b1, b2, rank, before):
                self.n, self.rounds, self.gw, self.gb, self.w1 = n, rounds, gw, gb, w1
                self.w2, self.b1, self.b2, self.rank, self.before = w2, b1, b2, rank, before
                self.links_per_group = 0
                self.copied = sem(name + "_copied")
                self.turned = sem(name + "_turned")
                self.xT = sem(name + "_xT")
                self.proj = sem(name + "_proj")
                self.vt = sem(name + "_vt")
                self.cos = sem(name + "_cos")
                self.norms = sem(name + "_norms")
                self.rn = sem(name + "_rn")
                self.diag = sem(name + "_diag")
                self.R = sem(name + "_R")
                self.x1 = sem(name + "_x1")
                self.T1 = sem(name + "_T1")
                self.x1T = sem(name + "_x1T")
                self.logits = sem(name + "_logits")
                self.lg = sem(name + "_lg")
                self.exp = sem(name + "_exp")
                self.up = sem(name + "_up")
                self.h = sem(name + "_h")
                self.down = sem(name + "_down")
                self.acc = sem(name + "_acc")
                self.coef = sem(name + "_coef")
                self.cT = sem(name + "_cT")
                self.cTs = sem(name + "_cTs")
                self.b2s = sem(name + "_b2s")
                self.boost = sem(name + "_boost")
                self.boostT = sem(name + "_boostT")
                self.boostTs = sem(name + "_boostTs")
                self.mv = sem(name + "_mv")
                self.ve = sem(name + "_ve")
                self.rstd = sem(name + "_rstd")
                self.x = sem(name + "_x")
                self.out = sem(name + "_out")
                self.links = sem(name + "_links")

        first = Attention("a0", w_qkv[:, 0:C], w_qkv[:, C:2 * C], w_qkv[:, 2 * C:3 * C], w_out0[:],
                          bq0, bk0, bv0, bo0, True, False, None)
        ffn0 = Experts("f0", E0, 2, gate_w0, gate_b0, w1_0, w2_0, b1_0, b2_0, rank0, (first.x, B))
        second = Attention("a1", wT[:, 2, :], wT[:, 3, :], wT[:, 4, :], wT[:, 5, :],
                           zero_col, zero_col, zero_row, zero_row, True, False, (ffn0.x, NG))
        third = Attention("a2", wqx[:], wkx[:], wvx[:], wox[:],
                          bq1, bk1, bv1, bo1, False, True, (second.x, B))
        ffn1 = Experts("f1", E1, 1, gate_w1, None, w1_1, w2_1, b1_1, b2_1, rank1, (third.x, B))

        def sequences(eng, step):
            for i in range(-1, 4):
                step(i, i % 2)
            with eng.Fori(4, B - 2, 2) as i:
                step(i, 0)
                step(i + 1, 1)
            for i in range(B - 2, B + 2):
                step(i, i % 2)

        def groups(eng, step):
            step(0)
            with eng.Fori(1, NG, 1) as i:
                step(i)

        def slot(g, n):
            return g % n

        def attention_pe(pe, p):
            if p.before:
                pe.wait_ge(*p.before)

            def scores(i, g, par):
                if not real(i, B):
                    return
                u = 4 * i + g
                if g == 0:
                    need(pe, p.q, i + 1)
                    need(pe, p.k, i + 1)
                need(pe, p.shifted, u - 1)
                dst = bank[slot(g, 2)]
                if p.masked:
                    nc.tensor.matmul(dst[:], ident_b[:], causal_b[:].rearrange("p a b -> p (a b)"),
                                     start=True, stop=False)
                nc.tensor.matmul(dst[:], qg[:, par, g, :], kj[:, par].rearrange("p a b -> p (a b)"),
                                 start=not p.masked, stop=True).then_inc(p.scores, 1)

            def turn(u, i, g):
                if not real(i, B):
                    return
                need(pe, p.exp, u + 1)
                need(pe, p.probsT, u - 1)
                for j in range(HU):
                    last = nc.tensor.transpose(bank[2 + slot(g, 2)][:, j * 128:(j + 1) * 128],
                                               probs[:, g, j, :], ident[:])
                last.then_inc(p.pT, 1)

            def values(u, i, g, par):
                if not real(i, B):
                    return
                need(pe, p.probsT, u + 1)
                if g == 0:
                    need(pe, p.v, i + 1)
                    need(pe, p.oT, i - 1)
                half = g // 2
                for j in range(HU):
                    h = g * HU + j
                    last = nc.tensor.matmul(bank[4 + par][:, half * 128:(half + 1) * 128],
                                            v_pad[:, par, 128 * h:128 * h + 128], probsT[:, slot(g, 2), j, :],
                                            start=(h % 8 == 0), stop=(h % 8 == 7))
                last.then_inc(p.pv, 1)

            def step(i, par):
                for g in range(UN):
                    scores(i, g, par)
                    if g == 0:
                        if real(i - 2, B):
                            need(pe, p.oT, i - 1)
                            need(pe, p.y, i - 2)
                            nc.tensor.matmul(bank[7][:, 0:128], oT[:, par, :], p.wo,
                                             start=True, stop=True).then_inc(p.proj, 1)
                        if real(i + 1, B):
                            n = 1 - par
                            need(pe, p.copied, i + 2)
                            need(pe, p.v, i + 1)
                            need(pe, p.k, i + 1)
                            need(pe, p.q, i + 1)
                            last = nc.tensor.transpose(bank[6][:, 384:512], xs[:, n, :], ident[:])
                            if p.cross:
                                last = nc.tensor.transpose(bank[6][0:CTX, 256:384], cs[:, n, :], ident[:])
                            last.then_inc(p.turned, 1)
                    if g == 1 and real(i + 1, B):
                        n = 1 - par
                        need(pe, p.xT, i + 2)
                        src = cT[:, n, :] if p.cross else xT[:, n, :]
                        nc.tensor.matmul(bank[6][:, 0:128], p.wq, xT[:, n, :], start=True, stop=True)
                        nc.tensor.matmul(bank[6][:, 128:256], p.wk, src, start=True, stop=True)
                        nc.tensor.matmul(bank[6][:, 256:384], src, p.wv, start=True,
                                         stop=True).then_inc(p.qkv, 1)
                    b2, g2 = (i, g - 2) if g >= 2 else (i - 1, g + 2)
                    turn(4 * i + g - 2, b2, g2)
                    b3, g3 = (i, g - 3) if g >= 3 else (i - 1, g + 1)
                    values(4 * i + g - 3, b3, g3, par if g >= 3 else 1 - par)

            sequences(pe, step)

        def attention_act(act, p):
            if p.before:
                act.wait_ge(*p.before)

            def step(i, par):
                for g in range(UN):
                    if g == 0 and real(i + 1, B):
                        n = 1 - par
                        act.wait_ge(p.turned, i + 2)
                        need(act, p.qkv, i)
                        if p.cross:
                            nc.scalar.activation(cT[:, n, :], bank[6][0:CTX, 256:384], ACT.Copy)
                        nc.scalar.activation(xT[:, n, :], bank[6][:, 384:512], ACT.Copy).then_inc(p.xT, 1)
                    b2, g2 = (i, g - 2) if g >= 2 else (i - 1, g + 2)
                    if real(b2, B):
                        u = 4 * i + g - 2
                        act.wait_ge(p.pT, u + 1)
                        need(act, p.pv, u - 1)
                        nc.scalar.activation(probsT[:, slot(g2, 2)].rearrange("p a b -> p (a b)"),
                                             bank[2 + slot(g2, 2)][:], ACT.Copy).then_inc(p.probsT, 1)
                    if real(i, B):
                        u = 4 * i + g
                        act.wait_ge(p.shifted, u + 1)
                        need(act, p.pT, u - 3)
                        nc.scalar.activation(probs[:, g], shifted[:, slot(g, 2)], ACT.Exp).then_inc(p.exp, 1)

            sequences(act, step)

        def attention_dve(dve, p):
            if p.before:
                dve.wait_ge(*p.before)

            def step(i, par):
                n = 1 - par
                for g in range(UN):
                    if real(i, B):
                        u = 4 * i + g
                        sc = bank[slot(g, 2)][:].rearrange("p (a b) -> p a b", a=HU)
                        dve.wait_ge(p.scores, u + 1)
                        nc.vector.reduce_max(mx[:, g, :], sc, AX).then_inc(p.max, 1)
                        dve.wait_ge(p.max, u + 1)
                        need(dve, p.exp, u - 1)
                        nc.vector.tensor_tensor(shifted[:, slot(g, 2)], sc,
                                                mx[:, g, :].unsqueeze(2).broadcast_to([128, HU, 128]),
                                                ALU.subtract).then_inc(p.shifted, 1)
                    if g == 1 and real(i - 2, B):
                        dve.wait_ge(p.proj, i - 1)
                        dve.wait_ge(p.res, i - 1)
                        nc.vector.tensor_tensor(y[:, par, :], bank[7][:, 0:128], xb[:, par, :],
                                                ALU.add).then_inc(p.y, 1)
                        dve.wait_ge(p.y, i - 1)
                        nc.vector.bn_stats(st[:, par, :], y[:, par, :])
                        dve.drain()
                        nc.vector.bn_aggr(mv[:, par, :], st[:, par, :]).then_inc(p.mv, 1)
                    if g == 1 and real(i + 1, B):
                        dve.wait_ge(p.qkv, i + 2)
                        need(dve, p.scores, 4 * i)
                        nc.vector.scalar_tensor_tensor(
                            qg[:, n], bank[6][:, 0:128].unsqueeze(1).broadcast_to([128, UN, 128]), p.bq[:, 0:1],
                            sel_q[:], ALU.add, ALU.mult).then_inc(p.q, 1)
                        nc.vector.scalar_tensor_tensor(
                            kj[:, n], bank[6][:, 128:256].unsqueeze(1).broadcast_to([128, HU, 128]), p.bk[:, 0:1],
                            sel_k[:], ALU.add, ALU.mult).then_inc(p.k, 1)
                    if g == 2 and real(i + 1, B):
                        need(dve, p.pv, 4 * i)
                        nc.vector.tensor_tensor(
                            v_pad[:, n, :].rearrange("p (a b c) -> p a b c", a=2, b=8)[:, :, :, 0:D],
                            bank[6][:, 256:384].rearrange("p (a b c) -> p a b c", a=2, b=8),
                            p.bv[:].rearrange("p (a b c) -> p a b c", a=2, b=8), ALU.add).then_inc(p.v, 1)
                    if g == 2 and real(i - 2, B):
                        dve.wait_ge(p.rstd, i - 1)
                        nc.vector.tensor_scalar(x_all[:, bass.ts(i - 2, C)], y[:, par, :], mv[:, par, 0:1],
                                                rs[:, par, :], ALU.subtract, ALU.mult).then_inc(p.x, 1)
                    if g == 3 and real(i - 1, B):
                        dve.wait_ge(p.pv, 4 * i)
                        o = bank[4 + n]
                        nc.vector.reciprocal(rden[0:64, n, :], o[64:128, 0:128])
                        nc.vector.reciprocal(rden[64:128, n, :], o[0:64, 128:256]).then_inc(p.rden, 1)
                        dve.wait_ge(p.rden, i)
                        need(dve, p.proj, i - 2)
                        nc.vector.tensor_tensor(oT[0:64, n, :], o[0:64, 0:128], rden[0:64, n, :], ALU.mult)
                        nc.vector.tensor_tensor(oT[64:128, n, :], o[64:128, 128:256], rden[64:128, n, :],
                                                ALU.mult).then_inc(p.oT, 1)

            sequences(dve, step)

        def attention_pool(pool, p):
            if p.before:
                pool.wait_ge(*p.before)

            def step(i, par):
                if real(i + 1, B):
                    n = 1 - par
                    need(pool, p.turned, i)
                    if p.cross:
                        nc.gpsimd.tensor_copy(cs[:, n, :], ctx_all[:, bass.ts(i + 1, CTX)])
                    nc.gpsimd.tensor_copy(xs[:, n, :], x_all[:, bass.ts(i + 1, C)]).then_inc(p.copied, 1)
                if real(i - 2, B):
                    need(pool, p.y, i - 3)
                    nc.gpsimd.tensor_tensor(xb[:, par, :], x_all[:, bass.ts(i - 2, C)], p.bo[:],
                                            ALU.add).then_inc(p.res, 1)
                    pool.wait_ge(p.mv, i - 1)
                    nc.gpsimd.tensor_tensor(ve[:, par, :], mv[:, par, 1:2], ln_eps[:, 0:1], ALU.add).then_inc(p.ve, 1)
                    pool.wait_ge(p.ve, i - 1)
                    nc.gpsimd.tensor_tensor(rs[:, par, :], ve[:, par, :], minus_half[:, 0:1],
                                            ALU.pow).then_inc(p.rstd, 1)

            sequences(pool, step)

        def norms_of(p):
            return 3 if p is ffn0 else 1

        def experts_pe(pe, p):
            cosine = p is ffn0
            pe.wait_ge(*p.before)

            def step(i):
                if cosine:
                    pe.wait_ge(p.copied, i + 1)
                    need(pe, p.x, i)
                    for b in range(GB):
                        nc.tensor.transpose(bank[0][:, b * 128:(b + 1) * 128], xg[:, b, :], ident[:])
                    for b in range(GB):
                        last = nc.tensor.transpose(bank[1][0:CTX, b * 128:(b + 1) * 128], cg[:, b, :], ident[:])
                    last.then_inc(p.turned, 1)
                    pe.wait_ge(p.xT, i + 1)
                    nc.tensor.matmul(bank[2][0:XH, :], wT[:, 0, 0:XH], xgT[:], start=True, stop=True)
                    nc.tensor.matmul(bank[3][0:XH, :], wT[0:CTX, 1, 0:XH], cgT[:], start=True,
                                     stop=True).then_inc(p.proj, 1)
                    pe.wait_ge(p.vt, i + 1)
                    for b in range(GB):
                        c = slice(b * 128, (b + 1) * 128)
                        nc.tensor.matmul(bank[4][:, c], vT[:, c], tT[:, c], start=True, stop=True)
                    for b in range(GB):
                        c = slice(b * 128, (b + 1) * 128)
                        nc.tensor.matmul(bank[6][:, b:b + 1], vT2[:, c], ones[0:XH, 0:1], start=True, stop=True)
                        last = nc.tensor.matmul(bank[6][:, GB + b:GB + b + 1], tT2[:, c], ones[0:XH, 0:1],
                                                start=True, stop=True)
                    last.then_inc(p.cos, 1)
                    pe.wait_ge(p.diag, i + 1)
                    nc.tensor.matmul(bank[5][:], ones[:], diag[:].rearrange("p a b -> p (a b)"),
                                     start=True, stop=True).then_inc(p.R, 1)
                    pe.wait_ge(p.x1, i + 1)
                else:
                    pe.wait_ge(p.copied, i + 1)
                    need(pe, p.x, i)
                for b in range(GB):
                    last = nc.tensor.transpose(bank[6][:, b * 128:(b + 1) * 128], xg[:, b, :], ident[:])
                last.then_inc(p.T1, 1)
                pe.wait_ge(p.x1T, i + 1)
                for b in range(GB):
                    last = nc.tensor.matmul(bank[7][:, b * p.n:(b + 1) * p.n], xgT[:, b * 128:(b + 1) * 128],
                                            p.gw[:], start=True, stop=True)
                last.then_inc(p.logits, 1)

                def up(r, e):
                    k = (i * p.rounds + r) * p.n + e
                    src = xgT if r == 0 else boostT
                    need(pe, p.h, 2 * (k - 1))
                    for c in range(2):
                        nc.tensor.matmul(bank[2 * (e % 2) + c][:], p.w1[:, e, c * 128:(c + 1) * 128], src[:],
                                         start=True, stop=True).then_inc(p.up, 1)

                def down(r, e):
                    k = (i * p.rounds + r) * p.n + e
                    pe.wait_ge(p.h, 2 * (k + 1))
                    need(pe, p.acc, k - 1)
                    for b in range(GB):
                        for c in range(2):
                            last = nc.tensor.matmul(bank[4 + e % 2][:, b * 128:(b + 1) * 128],
                                                    hid[:, e % 2, c, b * 128:(b + 1) * 128], p.w2[:, e, c, :],
                                                    start=(c == 0), stop=(c == 1))
                    last.then_inc(p.down, 1)

                for r in range(p.rounds):
                    up(r, 0)
                    for e in range(p.n):
                        if e + 1 < p.n:
                            up(r, e + 1)
                        down(r, e)
                    q = i * p.rounds + r
                    pe.wait_ge(p.coef, q + 1)
                    for b in range(GB):
                        last = nc.tensor.transpose(bank[6][:, b * 128:(b + 1) * 128], cpad[:, b, :], ident[:])
                    last.then_inc(p.cT, 1)
                    pe.wait_ge(p.cTs, q + 1)
                    for b in range(GB):
                        last = nc.tensor.matmul(bank[7][:, b * 128:(b + 1) * 128], cpT[:, b, :], p.b2[:],
                                                start=True, stop=True)
                    last.then_inc(p.b2s, 1)
                    if p.rounds == 2 and r == 0:
                        pe.wait_ge(p.boost, i + 1)
                        for b in range(GB):
                            last = nc.tensor.transpose(bank[6][:, b * 128:(b + 1) * 128], yg[:, b, :], ident[:])
                        last.then_inc(p.boostT, 1)
                        pe.wait_ge(p.boostTs, i + 1)

            groups(pe, step)

        def experts_act(act, p):
            cosine = p is ffn0
            act.wait_ge(*p.before)

            def step(i):
                if cosine:
                    act.wait_ge(p.turned, i + 1)
                    nc.scalar.activation(xgT[:], bank[0][:], ACT.Copy)
                    nc.scalar.activation(cgT[:], bank[1][0:CTX, :], ACT.Copy).then_inc(p.xT, 1)
                    act.wait_ge(p.proj, i + 1)
                    nc.scalar.activation(vT[:], bank[2][0:XH, :], ACT.Identity, bias=bvx[:, 0:1])
                    nc.scalar.activation(vT2[:], bank[2][0:XH, :], ACT.Square, bias=bvx[:, 0:1])
                    nc.scalar.activation(tT[:], bank[3][0:XH, :], ACT.Identity, bias=btx[:, 0:1])
                    nc.scalar.activation(tT2[:], bank[3][0:XH, :], ACT.Square, bias=btx[:, 0:1]).then_inc(p.vt, 1)
                act.wait_ge(p.T1, i + 1)
                nc.scalar.activation(xgT[:], bank[6][:], ACT.Copy).then_inc(p.x1T, 1)
                act.wait_ge(p.lg, i + 1)
                nc.scalar.activation(pr[:, :, 0:p.n], lg[:, :, 0:p.n], ACT.Exp).then_inc(p.exp, 1)
                for r in range(p.rounds):
                    for e in range(p.n):
                        k = (i * p.rounds + r) * p.n + e
                        need(act, p.down, k - 1)
                        for c in range(2):
                            act.wait_ge(p.up, 2 * k + c + 1)
                            nc.scalar.activation(hid[:, e % 2, c, :], bank[2 * (e % 2) + c][:], ACT.Relu,
                                                 bias=p.b1[:, 2 * e + c:2 * e + c + 1]).then_inc(p.h, 1)
                    q = i * p.rounds + r
                    act.wait_ge(p.cT, q + 1)
                    nc.scalar.activation(cpT[:].rearrange("p a b -> p (a b)"), bank[6][:],
                                         ACT.Copy).then_inc(p.cTs, 1)
                    if p.rounds == 2 and r == 0:
                        act.wait_ge(p.boostT, i + 1)
                        nc.scalar.activation(boostT[:], bank[6][:], ACT.Copy).then_inc(p.boostTs, 1)

            groups(act, step)

        def experts_dve(dve, p):
            cosine = p is ffn0
            dve.wait_ge(*p.before)
            n = p.n
            s_link = p.links

            def step(i):
                links = [0]

                def link(ins):
                    links[0] += 1
                    ins.then_inc(s_link, 1)
                    dve.wait_ge(s_link, i * p.links_per_group + links[0])

                def wide(t):
                    return t.unsqueeze(2).broadcast_to([128, GB, n])

                def layer_norm(src, dst, k, last=None):
                    m = i * norms_of(p) + k
                    for b in range(GB):
                        nc.vector.bn_stats(gst[:, b, :], src[:, b, :])
                    dve.drain()
                    for b in range(GB):
                        ins = nc.vector.bn_aggr(gmv[:, b, :], gst[:, b, :])
                    ins.then_inc(p.mv, 1)
                    dve.wait_ge(p.rstd, m + 1)
                    for b in range(GB):
                        ins = nc.vector.tensor_scalar(dst[:, b, :], src[:, b, :], gmv[:, b, 0:1],
                                                      grs[:, b:b + 1], ALU.subtract, ALU.mult)
                    return ins

                if cosine:
                    dve.wait_ge(p.cos, i + 1)
                    nc.vector.tensor_scalar(nrm[:], bank[6][:, 0:2 * GB], NORM_FLOOR, None,
                                            ALU.max).then_inc(p.norms, 1)
                    dve.wait_ge(p.rn, i + 1)
                    for b in range(GB):
                        ins = nc.vector.tensor_scalar(diag[:, b, :], ident[:], rn[:, GB + b:GB + b + 1], None, ALU.mult)
                    ins.then_inc(p.diag, 1)
                    dve.wait_ge(p.R, i + 1)
                    for b in range(GB):
                        ins = nc.vector.tensor_scalar(cosw[:, b, :], bank[5][:, b * 128:(b + 1) * 128],
                                                      rn[:, b:b + 1], 1.0 / COS_EPS, ALU.mult, ALU.min)
                    link(ins)
                    link(nc.vector.tensor_tensor(cosw[:], bank[4][:].rearrange("p (a b) -> p a b", a=GB),
                                                 cosw[:], ALU.mult))
                    link(nc.vector.tensor_tensor(yg[:], cosw[:], xg[:], ALU.add))
                    layer_norm(yg, xg, 0).then_inc(p.x1, 1)
                    dve.wait_ge(p.x1, i + 1)
                dve.wait_ge(p.logits, i + 1)
                logits = bank[7][:, 0:GB * n].rearrange("p (a b) -> p a b", a=GB)
                if p.gb is not None:
                    link(nc.vector.tensor_tensor(left[:, :, 0:n], logits,
                                                 p.gb[:].unsqueeze(1).broadcast_to([128, GB, n]), ALU.add))
                else:
                    link(nc.vector.tensor_copy(left[:, :, 0:n], logits))
                link(nc.vector.reduce_max(sm[:], left[:, :, 0:n], AX))
                nc.vector.tensor_tensor(lg[:, :, 0:n], left[:, :, 0:n], wide(sm[:]), ALU.subtract).then_inc(p.lg, 1)
                dve.wait_ge(p.exp, i + 1)
                link(nc.vector.reduce_sum(sm[:], pr[:, :, 0:n], AX))
                link(nc.vector.reciprocal(sm2[:], sm[:]))
                link(nc.vector.tensor_tensor(left[:, :, 0:n], pr[:, :, 0:n], wide(sm2[:]), ALU.mult))
                link(nc.vector.tensor_copy(pr[:, :, 0:n], left[:, :, 0:n]))

                def best(dst):
                    link(nc.vector.reduce_max(sm[:], left[:, :, 0:n], AX))
                    link(nc.vector.tensor_tensor(hot[:, :, 0:n], left[:, :, 0:n], wide(sm[:]), ALU.is_equal))
                    link(nc.vector.tensor_tensor(hot[:, :, 0:n], hot[:, :, 0:n],
                                                 p.rank[:].unsqueeze(1).broadcast_to([128, GB, n]), ALU.mult))
                    link(nc.vector.reduce_max(sm2[:], hot[:, :, 0:n], AX))
                    link(nc.vector.tensor_tensor(dst[:, :, 0:n], hot[:, :, 0:n], wide(sm2[:]), ALU.is_equal))
                    link(nc.vector.scalar_tensor_tensor(left[:, :, 0:n], dst[:, :, 0:n], -2.0, left[:, :, 0:n],
                                                        ALU.mult, ALU.add))

                if p.rounds == 2:
                    best(coef1)
                    link(nc.vector.tensor_copy(g1[:], sm[:]))
                    best(coef2)
                    link(nc.vector.tensor_tensor(coef2[:, :, 0:n], coef2[:, :, 0:n], pr[:, :, 0:n], ALU.mult))
                else:
                    best(coef1)
                    best(coef2)
                    link(nc.vector.tensor_tensor(coef1[:, :, 0:n], coef1[:, :, 0:n], coef2[:, :, 0:n], ALU.add))
                    best(coef2)
                    link(nc.vector.tensor_tensor(coef1[:, :, 0:n], coef1[:, :, 0:n], coef2[:, :, 0:n], ALU.add))
                    link(nc.vector.tensor_tensor(coef1[:, :, 0:n], coef1[:, :, 0:n], pr[:, :, 0:n], ALU.mult))
                    link(nc.vector.reduce_sum(sm[:], coef1[:, :, 0:n], AX))
                    link(nc.vector.tensor_scalar(sm[:], sm[:], 1e-12, None, ALU.max))
                    link(nc.vector.reciprocal(sm2[:], sm[:]))
                    link(nc.vector.tensor_tensor(coef1[:, :, 0:n], coef1[:, :, 0:n], wide(sm2[:]), ALU.mult))

                for r in range(p.rounds):
                    coef = coef1 if r == 0 else coef2
                    q = i * p.rounds + r
                    need(dve, p.cT, q)
                    nc.vector.tensor_copy(cpad[:, :, 0:n], coef[:, :, 0:n]).then_inc(p.coef, 1)
                    for e in range(n):
                        k = q * n + e
                        dve.wait_ge(p.down, k + 1)
                        need(dve, p.acc, k)
                        for b in range(GB):
                            o = bank[4 + e % 2][:, b * 128:(b + 1) * 128]
                            if e == 0:
                                ins = nc.vector.tensor_scalar(acc[:, b, :], o, coef[:, b, e:e + 1], None, ALU.mult)
                            else:
                                ins = nc.vector.scalar_tensor_tensor(acc[:, b, :], o, coef[:, b, e:e + 1],
                                                                     acc[:, b, :], ALU.mult, ALU.add)
                        ins.then_inc(p.acc, 1)
                    dve.wait_ge(p.b2s, q + 1)
                    dve.wait_ge(p.acc, (q + 1) * n)
                    bias = bank[7][:].rearrange("p (a b) -> p a b", a=GB)
                    if p.rounds == 2 and r == 0:
                        link(nc.vector.tensor_tensor(eo1[:], bias, acc[:], ALU.add))
                        nc.vector.scalar_tensor_tensor(yg[:], eo1[:], 0.5, xg[:], ALU.mult,
                                                       ALU.add).then_inc(p.boost, 1)
                if p.rounds == 2:
                    link(nc.vector.tensor_tensor(acc[:], bias, acc[:], ALU.add))
                    for b in range(GB):
                        ins = nc.vector.scalar_tensor_tensor(acc[:, b, :], eo1[:, b, :], g1[:, b:b + 1],
                                                             acc[:, b, :], ALU.mult, ALU.add)
                    link(ins)
                    link(nc.vector.tensor_tensor(acc[:], acc[:], xg[:], ALU.add))
                    link(layer_norm(acc, yg, 1))
                    link(nc.vector.tensor_tensor(yg[:], yg[:], gamma[:].unsqueeze(1).broadcast_to([128, GB, C]),
                                                 ALU.mult))
                    link(nc.vector.tensor_tensor(yg[:], yg[:], beta[:].unsqueeze(1).broadcast_to([128, GB, C]),
                                                 ALU.add))
                    link(nc.vector.tensor_tensor(yg[:], yg[:], xg[:], ALU.add))
                    layer_norm(yg, acc, 2).then_inc(s_link, 1)
                    links[0] += 1
                    dve.wait_ge(s_link, i * p.links_per_group + links[0])
                    nc.vector.tensor_copy(x_all[:, bass.ts(i, GB * C)],
                                          acc[:].rearrange("p a b -> p (a b)")).then_inc(p.x, 1)
                else:
                    link(nc.vector.tensor_tensor(acc[:], bias, acc[:], ALU.add))
                    link(nc.vector.tensor_tensor(acc[:], acc[:], xg[:], ALU.add))
                    need(dve, p.out, 16 * i)
                    layer_norm(acc, xo, 0).then_inc(p.x, 1)
                p.links_per_group = links[0]

            groups(dve, step)

        def experts_pool(pool, p):
            cosine = p is ffn0
            pool.wait_ge(*p.before)

            def step(i):
                need(pool, p.x, i)
                if cosine:
                    nc.gpsimd.tensor_copy(cg[:].rearrange("p a b -> p (a b)"), ctx_all[:, bass.ts(i, GB * CTX)])
                nc.gpsimd.tensor_copy(xg[:].rearrange("p a b -> p (a b)"),
                                      x_all[:, bass.ts(i, GB * C)]).then_inc(p.copied, 1)
                if cosine:
                    pool.wait_ge(p.norms, i + 1)
                    nc.gpsimd.tensor_tensor(rn[:], nrm[:], minus_half[:], ALU.pow).then_inc(p.rn, 1)
                for k in range(norms_of(p)):
                    m = i * norms_of(p) + k
                    pool.wait_ge(p.mv, m + 1)
                    nc.gpsimd.tensor_tensor(gve[:], gmv[:, :, 1], ln_eps[:], ALU.add).then_inc(p.ve, 1)
                    pool.wait_ge(p.ve, m + 1)
                    nc.gpsimd.tensor_tensor(grs[:], gve[:], minus_half[:, 0:GB], ALU.pow).then_inc(p.rstd, 1)

            groups(pool, step)

        block = ctx.enter_context(nc.Block())

        @block.sync
        def _(sp):
            for dst, src in small_in:
                sp.dma_start(dst, src).then_inc(s_in, 16)
            def step(i):
                sp.wait_ge(ffn1.x, i + 1)
                sp.dma_start(out[bass.ts(i, GB), :, :].rearrange("b p c -> p b c"), xo[:]).then_inc(ffn1.out, 16)

            groups(sp, step)
            sp.wait_ge(ffn1.out, 16 * NG)

        @block.tensor
        def _(pe):
            pe.wait_ge(s_in, 16 * len(small_in))
            pe.wait_ge(s_const, CONSTS)
            for k, (rows, cols) in enumerate(TURNED):
                last = nc.tensor.transpose(bank[k // 3][0:cols, (k % 3) * 128:(k % 3) * 128 + rows],
                                           raw[0:rows, k, 0:cols], ident[0:rows, 0:rows])
            last.then_inc(s_rawT, 1)
            pe.wait_ge(s_wT, 1)
            attention_pe(pe, first)
            pe.wait_ge(s_w, LATE)
            pe.wait_ge(s_b2, 16 * len(padded_in))
            experts_pe(pe, ffn0)
            attention_pe(pe, second)
            attention_pe(pe, third)
            experts_pe(pe, ffn1)

        @block.scalar
        def _(act):
            for dst, src in late_in:
                act.dma_start(dst, src).then_inc(s_w, 16)
            act.wait_ge(s_rawT, 1)
            for k, (rows, cols) in enumerate(TURNED):
                last = nc.scalar.activation(wT[0:cols, k, 0:rows],
                                            bank[k // 3][0:cols, (k % 3) * 128:(k % 3) * 128 + rows], ACT.Copy)
            last.then_inc(s_wT, 1)
            attention_act(act, first)
            act.wait_ge(s_w, LATE)
            experts_act(act, ffn0)
            attention_act(act, second)
            attention_act(act, third)
            experts_act(act, ffn1)

        @block.vector
        def _(dve):
            nc.vector.memset(v_pad[:].rearrange("p a b -> p (a b)"), 0.0).then_inc(s_const, 1)
            nc.vector.memset(ones[:], 1.0).then_inc(s_const, 1)
            nc.vector.memset(minus_half[:], -0.5).then_inc(s_const, 1)
            nc.vector.memset(zero_col[:], 0.0).then_inc(s_const, 1)
            nc.vector.memset(zero_row[:], 0.0).then_inc(s_const, 1)
            nc.vector.memset(cpad[:], 0.0).then_inc(s_const, 1)
            nc.vector.memset(ln_eps[:], LN_EPS).then_inc(s_const, 1)
            dve.wait_ge(s_const, 7)
            for par in range(2):
                for half in range(2):
                    at = 64 if half == 0 else 1024
                    nc.vector.memset(v_pad[:, par, at:at + HALF].rearrange("p (b c) -> p b c", c=136)[:, :, 0:D],
                                     1.0).then_inc(s_const, 1)
            dve.wait_ge(s_in, 16 * len(small_in))
            nc.vector.tensor_copy(ident_b[:], ident[:])
            nc.vector.tensor_copy(causal_b[:], causal[:].unsqueeze(1).broadcast_to([128, HU, 128]))
            nc.vector.tensor_copy(sel_q[:], sel[:, 0, :].unsqueeze(2).broadcast_to([128, UN, 128]))
            nc.vector.tensor_copy(sel_k[:], sel[:, 1, :].unsqueeze(2).broadcast_to([128, HU, 128])).then_inc(s_const, 1)
            dve.wait_ge(s_const, CONSTS)
            attention_dve(dve, first)
            dve.wait_ge(s_w, LATE)
            experts_dve(dve, ffn0)
            attention_dve(dve, second)
            attention_dve(dve, third)
            experts_dve(dve, ffn1)

        @block.gpsimd
        def _(pool):
            nc.gpsimd.memset(b2_0[:], 0.0).then_inc(s_zeroed, 1)
            nc.gpsimd.memset(b2_1[:], 0.0).then_inc(s_zeroed, 1)
            pool.wait_ge(s_zeroed, 2)
            for dst, src in padded_in:
                pool.dma_start(dst, src).then_inc(s_b2, 16)
            pool.wait_ge(s_const, CONSTS)
            pool.wait_ge(s_in, 16 * len(small_in))
            attention_pool(pool, first)
            pool.wait_ge(s_w, LATE)
            experts_pool(pool, ffn0)
            attention_pool(pool, second)
            attention_pool(pool, third)
            experts_pool(pool, ffn1)


_INS = ['x', 'ctx_768', 'L0_attn_w_qkv', 'L0_attn_b_qkv', 'L0_attn_w_out', 'L0_attn_b_out', 'L0_xattn_Wv',
        'L0_xattn_bv', 'L0_xattn_Wt', 'L0_xattn_bt', 'L0_ffn_gate_W', 'L0_ffn_gate_b', 'L0_ffn_W1', 'L0_ffn_b1',
        'L0_ffn_W2', 'L0_ffn_b2', 'L0_ffn_ln_gamma', 'L0_ffn_ln_beta', 'L1_attn_Wq', 'L1_attn_Wk', 'L1_attn_Wv',
        'L1_attn_Wo', 'L1_xattn_wq', 'L1_xattn_bq', 'L1_xattn_wk', 'L1_xattn_bk', 'L1_xattn_wv', 'L1_xattn_bv',
        'L1_xattn_wo', 'L1_xattn_bo', 'L1_ffn_gate', 'L1_ffn_W1', 'L1_ffn_b1', 'L1_ffn_W2', 'L1_ffn_b2']


def constants():
    p = np.arange(128)
    sel = np.zeros((128, 2, UN), np.float32)
    sel[:, 0, :] = (p[:, None] // (HU * D) == np.arange(UN)) * np.float32(D ** -0.5)
    sel[:, 1, :] = p[:, None] // D % HU == np.arange(HU)
    return {
        "ident": np.eye(128, dtype=np.float32),
        "causal": np.where(p[:, None] >= p[None, :], 0.0, -BIG).astype(np.float32),
        "sel": sel,
        "rank0": np.arange(E0, 0, -1).astype(np.float32),
        "rank1": np.arange(E1, 0, -1).astype(np.float32),
    }


def kernel(**inputs):
    import concourse.bacc as _bacc
    from concourse.bass_utils import run_bass_kernel_spmd as _run

    nc = _bacc.Bacc("TRN2", target_bir_lowering=False, num_devices=1)
    arrays, aps = {}, {}
    given = {name: np.ascontiguousarray(inputs[name]) for name in _INS}
    for name, v in {**given, **constants()}.items():
        arrays[f"in_{name}"] = v
        aps[name] = nc.dram_tensor(f"in_{name}", v.shape, mybir.dt.from_np(v.dtype), kind="ExternalInput").ap()
    out = nc.dram_tensor("out_0", (B, T, C), F32, kind="ExternalOutput").ap()
    decoder(nc, aps, out)
    r = _run(nc, [arrays], core_ids=[0])
    return r.results[0]["out_0"]
```

```python
import numpy as np
import concourse.bass as bass
from concourse import mybir
from contextlib import ExitStack

B, T, C, H = 16, 128, 128, 16
D = C // H
CTX = 96
XH = 64
FH = 256
E0, E1 = 8, 16
GB = 4
NG = B // GB
HU = 4
UN = H // HU
LN_EPS = 1e-5
COS_EPS = 1e-8
NORM_FLOOR = 1e-30
BIG = 1e30

F32 = mybir.dt.float32
BF16 = mybir.dt.bfloat16
ALU = mybir.AluOpType
ACT = mybir.ActivationFunctionType
AX = mybir.AxisListType.X


def need(eng, sem, value):
    if isinstance(value, int) and value <= 0:
        return
    eng.wait_ge(sem, value)


def real(b, n):
    return not isinstance(b, int) or 0 <= b < n


def decoder(nc, a, out):
    ctx = ExitStack()
    with ctx:
        def sb(name, shape, dt=F32):
            return ctx.enter_context(nc.sbuf_tensor(name, shape, dt))

        def sem(name):
            return ctx.enter_context(nc.semaphore(name))

        bank = [ctx.enter_context(nc.psum_tensor(f"bank{n}", [128, 512], F32)) for n in range(8)]

        x_all = sb("x_all", [128, B * C])
        ctx_all = sb("ctx_all", [128, B * CTX])
        ident = sb("ident", [128, 128])
        causal = sb("causal", [128, 128])
        sel = sb("sel", [128, 2, UN])
        sel_q = sb("sel_q", [128, UN, 128])
        sel_k = sb("sel_k", [128, HU, 128])
        ones = sb("ones", [128, 128])
        minus_half = sb("minus_half", [128, 2 * GB])
        ln_eps = sb("ln_eps", [128, GB])
        zero_col = sb("zero_col", [128, 1])
        zero_row = sb("zero_row", [128, 128])

        w_qkv = sb("w_qkv", [128, 3 * C])
        bq0 = sb("bq0", [128, 1])
        bk0 = sb("bk0", [128, 1])
        bv0 = sb("bv0", [128, C])
        w_out0 = sb("w_out0", [128, C])
        bo0 = sb("bo0", [128, C])

        raw = sb("raw", [128, 8, 128])
        wT = sb("wT", [128, 8, 128])
        b1_0 = wT[:, 6, 0:2 * E0]
        b1_1 = wT[:, 7, 0:2 * E1]
        bvx = sb("bvx", [XH, 1])
        btx = sb("btx", [XH, 1])

        wqx = sb("wqx", [128, C])
        wkx = sb("wkx", [CTX, C])
        wvx = sb("wvx", [CTX, C])
        wox = sb("wox", [128, C])
        bq1 = sb("bq1", [128, 1])
        bk1 = sb("bk1", [128, 1])
        bv1 = sb("bv1", [128, C])
        bo1 = sb("bo1", [128, C])

        gate_w0 = sb("gate_w0", [128, E0])
        gate_b0 = sb("gate_b0", [128, E0])
        gate_w1 = sb("gate_w1", [128, E1])
        gamma = sb("gamma", [128, C])
        beta = sb("beta", [128, C])
        w1_0 = sb("w1_0", [128, E0, FH])
        w2_0 = sb("w2_0", [128, E0, 2, C])
        w1_1 = sb("w1_1", [128, E1, FH])
        w2_1 = sb("w2_1", [128, E1, 2, C])
        b2_0 = sb("b2_0", [128, C])
        b2_1 = sb("b2_1", [128, C])
        rank0 = sb("rank0", [128, E0])
        rank1 = sb("rank1", [128, E1])

        xs = sb("xs", [128, 2, C])
        cs = sb("cs", [128, 2, CTX])
        xT = sb("xT", [128, 2, 128])
        cT = sb("cT", [CTX, 2, 128])
        qg = sb("qg", [128, 2, UN, 128])
        kj = sb("kj", [128, 2, HU, 128])
        HALF = 8 * 136
        v_pad = sb("v_pad", [128, 2, 2 * HALF])
        neg_max = sb("neg_max", [128, UN, HU])
        masked = sb("masked", [128, 2, HU, 128])
        probs = sb("probs", [128, 4, HU, 128])
        probsT = sb("probsT", [128, 2, HU, 128])
        o_raw = sb("o_raw", [128, 2, 256])
        rden = sb("rden", [128, 2, H])
        o_norm = sb("o_norm", [128, 2, C])
        oT = sb("oT", [128, 2, 128])
        xb = sb("xb", [128, 2, C])
        y = sb("y", [128, 2, C])
        st = sb("st", [128, 2, 6])
        mv = sb("mv", [128, 2, 2])
        ve = sb("ve", [128, 2, 1])
        rs = sb("rs", [128, 2, 1])

        xg = sb("xg", [128, 2, GB, C])
        cg = sb("cg", [128, 2, GB, CTX])
        xgT = sb("xgT", [128, 2, GB * 128])
        cgT = sb("cgT", [CTX, 2, GB * 128])
        cosine_T = sb("cosine_T", [128, 4, 2, GB * 128])
        vT, vT2, tT, tT2 = (cosine_T[0:XH, k] for k in range(4))
        nrm = sb("nrm", [128, 2, 2 * GB])
        rn = sb("rn", [128, 2, 2 * GB])
        diag = sb("diag", [128, 2, GB, 128])
        cosw = sb("cosw", [128, 2, GB, 128])
        yg = sb("yg", [128, 2, GB, C])
        gst = sb("gst", [128, 2, GB, 6])
        gmv = sb("gmv", [128, 2, GB, 2])
        gve = sb("gve", [128, 2, GB])
        grs = sb("grs", [128, 2, GB])
        in_T = sb("in_T", [128, B * 128])
        eo_all = cosine_T[:, 0:2].rearrange("p a b c -> p (a b c)")
        logit = sb("logit", [128, B * E1])
        pr = sb("pr", [128, B, E1])
        left = sb("left", [128, B, E1])
        hot = sb("hot", [128, B, E1])
        coef1 = sb("coef1", [128, B, E1])
        coef2 = sb("coef2", [128, B, E1])
        sm = sb("sm", [128, B])
        sm2 = sb("sm2", [128, B])
        g1 = sb("g1", [128, B])
        hid = probs[:].rearrange("p (a b) c d -> p a b (c d)", a=2)
        acc = sb("acc", [128, GB, C])
        cpad = sb("cpad", [128, GB, 128])
        cpT = sb("cpT", [128, GB, 128])
        total = sb("total", [128, GB, C])
        norm1 = sb("norm1", [128, GB, C])
        xo = sb("xo", [128, GB, C])

        s_in = sem("s_in")
        s_w = sem("s_w")
        s_const = sem("s_const")
        s_zeroed = sem("s_zeroed")
        s_b2 = sem("s_b2")
        s_rawT = sem("s_rawT")
        s_wT = sem("s_wT")

        small_in = [(ident[:], a["ident"]), (causal[:], a["causal"]), (sel[:], a["sel"]),
                    (x_all[:].rearrange("p (b c) -> p b c", b=B), a["x"].rearrange("b p c -> p b c")),
                    (w_qkv[:], a["L0_attn_w_qkv"]),
                    (bq0[:], a["L0_attn_b_qkv"][0:C].rearrange("(c o) -> c o", o=1)),
                    (bk0[:], a["L0_attn_b_qkv"][C:2 * C].rearrange("(c o) -> c o", o=1)),
                    (bv0[:], a["L0_attn_b_qkv"][2 * C:3 * C].partition_broadcast(128)),
                    (w_out0[:], a["L0_attn_w_out"]),
                    (bo0[:], a["L0_attn_b_out"].partition_broadcast(128)),
                    (raw[0:XH, 0, :], a["L0_xattn_Wv"]), (raw[0:XH, 1, 0:CTX], a["L0_xattn_Wt"]),
                    (raw[:, 2, :], a["L1_attn_Wq"]), (raw[:, 3, :], a["L1_attn_Wk"]),
                    (raw[:, 4, :], a["L1_attn_Wv"]), (raw[:, 5, :], a["L1_attn_Wo"]),
                    (raw[0:2 * E0, 6, :], a["L0_ffn_b1"].rearrange("e (k h) -> (e k) h", k=2)),
                    (raw[0:2 * E1, 7, :], a["L1_ffn_b1"].rearrange("e (k h) -> (e k) h", k=2))]
        TURNED = ((XH, C), (XH, CTX), (C, C), (C, C), (C, C), (C, C), (2 * E0, 128), (2 * E1, 128))
        late_in = [(ctx_all[:].rearrange("p (b c) -> p b c", b=B), a["ctx_768"].rearrange("b p c -> p b c")),
                   (bvx[:], a["L0_xattn_bv"].rearrange("(c o) -> c o", o=1)),
                   (btx[:], a["L0_xattn_bt"].rearrange("(c o) -> c o", o=1)),
                   (gate_w0[:], a["L0_ffn_gate_W"]), (gate_b0[:], a["L0_ffn_gate_b"].partition_broadcast(128)),
                   (rank0[:], a["rank0"].partition_broadcast(128)),
                   (w1_0[:], a["L0_ffn_W1"].rearrange("e c h -> c e h")),
                   (w2_0[:], a["L0_ffn_W2"].rearrange("e (k h) c -> h e k c", k=2)),
                   (gamma[:], a["L0_ffn_ln_gamma"].partition_broadcast(128)),
                   (beta[:], a["L0_ffn_ln_beta"].partition_broadcast(128)),
                   (wqx[:], a["L1_xattn_wq"]), (wkx[:], a["L1_xattn_wk"]),
                   (wvx[:], a["L1_xattn_wv"]), (wox[:], a["L1_xattn_wo"]),
                   (bq1[:], a["L1_xattn_bq"].rearrange("(c o) -> c o", o=1)),
                   (bk1[:], a["L1_xattn_bk"].rearrange("(c o) -> c o", o=1)),
                   (bv1[:], a["L1_xattn_bv"].partition_broadcast(128)),
                   (bo1[:], a["L1_xattn_bo"].partition_broadcast(128)),
                   (gate_w1[:], a["L1_ffn_gate"]), (rank1[:], a["rank1"].partition_broadcast(128)),
                   (w1_1[:], a["L1_ffn_W1"].rearrange("e c h -> c e h")),
                   (w2_1[:], a["L1_ffn_W2"].rearrange("e (k h) c -> h e k c", k=2))]
        padded_in = [(b2_0[0:E0, :], a["L0_ffn_b2"]), (b2_1[0:E1, :], a["L1_ffn_b2"])]
        LATE = 16 * len(late_in)
        CONSTS = 12

        class Attention:

            def __init__(self, name, wq, wk, wv, wo, bq, bk, bv, bo, causal, cross, before):
                self.wq, self.wk, self.wv, self.wo, self.bq = wq, wk, wv, wo, bq
                self.bk, self.bv, self.bo, self.causal, self.cross = bk, bv, bo, causal, cross
                self.before = before
                self.copied = sem(name + "_copied")
                self.turned = sem(name + "_turned")
                self.xT = sem(name + "_xT")
                self.qkv = sem(name + "_qkv")
                self.q = sem(name + "_q")
                self.k = sem(name + "_k")
                self.v = sem(name + "_v")
                self.scores = sem(name + "_scores")
                self.hidden = sem(name + "_hidden") if causal else None
                self.max = sem(name + "_max")
                self.exp = sem(name + "_exp")
                self.pT = sem(name + "_pT")
                self.probsT = sem(name + "_probsT")
                self.pv = sem(name + "_pv")
                self.o_raw = sem(name + "_o_raw")
                self.o_tok = sem(name + "_o_tok")
                self.rden = sem(name + "_rden")
                self.o_norm = sem(name + "_o_norm")
                self.o_back = sem(name + "_o_back")
                self.oT = sem(name + "_oT")
                self.proj = sem(name + "_proj")
                self.res = sem(name + "_res")
                self.y = sem(name + "_y")
                self.mv = sem(name + "_mv")
                self.rstd = sem(name + "_rstd")
                self.x = sem(name + "_x")

        class Gates:

            def __init__(self, name, n, w, b, rank, cosine, before):
                self.n, self.w, self.b, self.rank, self.cosine, self.before = n, w, b, rank, cosine, before
                self.copied = sem(name + "_copied")
                self.turned = sem(name + "_turned") if cosine else None
                self.xT = sem(name + "_xT") if cosine else None
                self.proj = sem(name + "_proj") if cosine else None
                self.vt = sem(name + "_vt") if cosine else None
                self.cos = sem(name + "_cos") if cosine else None
                self.norms = sem(name + "_norms") if cosine else None
                self.rn = sem(name + "_rn") if cosine else None
                self.diag = sem(name + "_diag") if cosine else None
                self.R = sem(name + "_R") if cosine else None
                self.sum = sem(name + "_sum") if cosine else None
                self.mv = sem(name + "_mv") if cosine else None
                self.rstd = sem(name + "_rstd") if cosine else None
                self.x1 = sem(name + "_x1") if cosine else None
                self.stored = sem(name + "_stored") if cosine else None
                self.T1 = sem(name + "_T1")
                self.x1T = sem(name + "_x1T")
                self.logits = sem(name + "_logits")
                self.kept = sem(name + "_kept")
                self.shifted = sem(name + "_shifted")
                self.exp = sem(name + "_exp")
                self.chain = sem(name + "_chain")

        class Round:

            def __init__(self, name, gates, w1, w2, b1, b2, coef, kind):
                self.gates, self.n, self.coef, self.kind = gates, gates.n, coef, kind
                self.w1, self.w2, self.b1, self.b2 = w1, w2, b1, b2
                self.up = sem(name + "_up")
                self.h = sem(name + "_h")
                self.down = sem(name + "_down")
                self.acc = sem(name + "_acc")
                self.padded = sem(name + "_padded")
                self.cT = sem(name + "_cT")
                self.cTs = sem(name + "_cTs")
                self.b2s = sem(name + "_b2s")
                self.total = sem(name + "_total")
                self.boost = sem(name + "_boost") if kind != "mix" else None
                self.boostT = sem(name + "_boostT") if kind == "boost" else None
                self.boostTs = sem(name + "_boostTs") if kind == "boost" else None
                self.tail = sem(name + "_tail") if kind != "boost" else None
                self.mv = sem(name + "_mv") if kind != "boost" else None
                self.rstd = sem(name + "_rstd") if kind != "boost" else None
                self.x = sem(name + "_x") if kind != "boost" else None
                self.out = sem(name + "_out") if kind == "mix" else None

        first = Attention("a0", w_qkv[:, 0:C], w_qkv[:, C:2 * C], w_qkv[:, 2 * C:3 * C], w_out0[:],
                          bq0, bk0, bv0, bo0, True, False, None)
        gates0 = Gates("g0", E0, gate_w0, gate_b0, rank0, True, (first.x, B))
        boosting = Round("r0", gates0, w1_0, w2_0, b1_0, b2_0, coef1, "boost")
        fusing = Round("r1", gates0, w1_0, w2_0, b1_0, b2_0, coef2, "fuse")
        second = Attention("a1", wT[:, 2, :], wT[:, 3, :], wT[:, 4, :], wT[:, 5, :],
                           zero_col, zero_col, zero_row, zero_row, True, False, (fusing.x, NG))
        third = Attention("a2", wqx[:], wkx[:], wvx[:], wox[:],
                          bq1, bk1, bv1, bo1, False, True, (second.x, B))
        gates1 = Gates("g1", E1, gate_w1, None, rank1, False, (third.x, B))
        mixing = Round("r2", gates1, w1_1, w2_1, b1_1, b2_1, coef1, "mix")

        def sequences(eng, step):
            for i in range(-2, 4):
                step(i, i % 2)
            with eng.Fori(4, B - 3, 2) as i:
                step(i, 0)
                step(i + 1, 1)
            for i in range(B - 2, B + 3):
                step(i, i % 2)

        def pairs(eng, step):
            for i in range(0, NG, 2):
                step(i)

        def groups(eng, step):
            step(0)
            with eng.Fori(1, NG, 1) as i:
                step(i)

        def slot(g, n):
            return g % n

        def attention_pe(pe, p):
            if p.before:
                pe.wait_ge(*p.before)

            def scores(i, g, par):
                u = 4 * i + g
                if g == 0:
                    need(pe, p.q, i + 1)
                    need(pe, p.k, i + 1)
                need(pe, p.hidden if p.causal else p.exp, u - 1)
                nc.tensor.matmul(bank[slot(g, 2)][:], qg[:, par, g, :], kj[:, par].rearrange("p a b -> p (a b)"),
                                 start=True, stop=True).then_inc(p.scores, 1)

            def turn(u, g):
                pe.wait_ge(p.exp, u + 1)
                need(pe, p.probsT, u - 1)
                for j in range(HU):
                    last = nc.tensor.transpose(bank[2 + slot(g, 2)][:, j * 128:(j + 1) * 128],
                                               probs[:, g, j, :], ident[:])
                last.then_inc(p.pT, 1)

            def values(u, i, g, par):
                pe.wait_ge(p.probsT, u + 1)
                if g == 0:
                    pe.wait_ge(p.v, i + 1)
                    need(pe, p.o_raw, i - 1)
                half = g // 2
                for j in range(HU):
                    h = g * HU + j
                    last = nc.tensor.matmul(bank[4 + par][:, half * 128:(half + 1) * 128],
                                            v_pad[:, par, 128 * h:128 * h + 128], probsT[:, slot(g, 2), j, :],
                                            start=(h % 8 == 0), stop=(h % 8 == 7))
                last.then_inc(p.pv, 1)

            def step(i, par):
                n = 1 - par
                for g in range(UN):
                    if real(i, B):
                        scores(i, g, par)
                    if g == 0:
                        if real(i + 1, B):
                            need(pe, p.copied, i + 2)
                            need(pe, p.v, i + 1)
                            need(pe, p.k, i + 1)
                            need(pe, p.q, i + 1)
                            last = nc.tensor.transpose(bank[6][:, 384:512], xs[:, n, :], ident[:])
                            if p.cross:
                                last = nc.tensor.transpose(bank[6][0:CTX, 256:384], cs[:, n, :], ident[:])
                            last.then_inc(p.turned, 1)
                        if real(i - 2, B):
                            pe.wait_ge(p.o_raw, i - 1)
                            need(pe, p.y, i - 2)
                            for half in range(2):
                                last = nc.tensor.transpose(bank[7][:, half * 128:(half + 1) * 128],
                                                           o_raw[:, par, half * 128:(half + 1) * 128], ident[:])
                            last.then_inc(p.o_tok, 1)
                    if g == 1:
                        if real(i + 1, B):
                            need(pe, p.xT, i + 2)
                            src = cT[:, n, :] if p.cross else xT[:, n, :]
                            nc.tensor.matmul(bank[6][:, 0:128], p.wq, xT[:, n, :], start=True, stop=True)
                            nc.tensor.matmul(bank[6][:, 128:256], p.wk, src, start=True, stop=True)
                            nc.tensor.matmul(bank[6][:, 256:384], src, p.wv, start=True,
                                             stop=True).then_inc(p.qkv, 1)
                        if real(i - 2, B):
                            pe.wait_ge(p.o_norm, i - 1)
                            nc.tensor.transpose(bank[7][:, 256:384], o_norm[:, par, :],
                                                ident[:]).then_inc(p.o_back, 1)
                    if g == 3 and real(i - 2, B):
                        pe.wait_ge(p.oT, i - 1)
                        nc.tensor.matmul(bank[7][:, 384:512], oT[:, par, :], p.wo,
                                         start=True, stop=True).then_inc(p.proj, 1)
                    b2, g2 = (i, g - 2) if g >= 2 else (i - 1, g + 2)
                    if real(b2, B):
                        turn(4 * i + g - 2, g2)
                    b3, g3 = (i, g - 3) if g >= 3 else (i - 1, g + 1)
                    if real(b3, B):
                        values(4 * i + g - 3, b3, g3, par if g >= 3 else n)

            sequences(pe, step)

        def attention_act(act, p):
            if p.before:
                act.wait_ge(*p.before)

            def step(i, par):
                n = 1 - par
                for g in range(UN):
                    if g == 0 and real(i + 1, B):
                        act.wait_ge(p.turned, i + 2)
                        need(act, p.qkv, i)
                        if p.cross:
                            nc.scalar.activation(cT[:, n, :], bank[6][0:CTX, 256:384], ACT.Copy)
                        nc.scalar.activation(xT[:, n, :], bank[6][:, 384:512], ACT.Copy).then_inc(p.xT, 1)
                    b2, g2 = (i, g - 2) if g >= 2 else (i - 1, g + 2)
                    if real(b2, B):
                        u = 4 * i + g - 2
                        act.wait_ge(p.pT, u + 1)
                        need(act, p.pv, u - 1)
                        nc.scalar.activation(probsT[:, slot(g2, 2)].rearrange("p a b -> p (a b)"),
                                             bank[2 + slot(g2, 2)][:], ACT.Copy).then_inc(p.probsT, 1)
                    if g == 1 and real(i - 2, B):
                        act.wait_ge(p.o_back, i - 1)
                        need(act, p.proj, i - 3)
                        nc.scalar.activation(oT[:, par, :], bank[7][:, 256:384], ACT.Copy).then_inc(p.oT, 1)
                    if real(i, B):
                        u = 4 * i + g
                        act.wait_ge(p.max, u + 1)
                        need(act, p.pT, u - 3)
                        for j in range(HU):
                            src = masked[:, slot(g, 2), j, :] if p.causal else \
                                bank[slot(g, 2)][:, j * 128:(j + 1) * 128]
                            ins = nc.scalar.activation(probs[:, g, j, :], src, ACT.Exp, bias=neg_max[:, g, j:j + 1])
                        ins.then_inc(p.exp, 1)
                    if g == 3 and real(i - 1, B):
                        act.wait_ge(p.pv, 4 * i)
                        need(act, p.o_tok, i - 2)
                        nc.scalar.activation(o_raw[:, n, :], bank[4 + n][:, 0:256], ACT.Copy).then_inc(p.o_raw, 1)

            sequences(act, step)

        def attention_dve(dve, p):
            if p.before:
                dve.wait_ge(*p.before)

            def step(i, par):
                n = 1 - par
                for g in range(UN):
                    if real(i, B):
                        u = 4 * i + g
                        sc = bank[slot(g, 2)][:].rearrange("p (a b) -> p a b", a=HU)
                        dve.wait_ge(p.scores, u + 1)
                        if p.causal:
                            need(dve, p.exp, u - 1)
                            nc.vector.tensor_tensor(masked[:, slot(g, 2)], sc,
                                                    causal[:].unsqueeze(1).broadcast_to([128, HU, 128]),
                                                    ALU.add).then_inc(p.hidden, 1)
                            dve.wait_ge(p.hidden, u + 1)
                            sc = masked[:, slot(g, 2)]
                        nc.vector.reduce_max(neg_max[:, g, :], sc, AX, negate=True).then_inc(p.max, 1)
                    if g == 0 and real(i - 2, B):
                        dve.wait_ge(p.o_tok, i - 1)
                        nc.vector.reciprocal(rden[:, par, :].unsqueeze(2), bank[7][:, 64:192].rearrange(
                            "p (h d) -> p h d", d=D)[:, :, 0:1]).then_inc(p.rden, 1)
                        dve.wait_ge(p.rden, i - 1)
                        need(dve, p.o_back, i - 3)
                        for half, at in ((0, 0), (1, 192)):
                            ins = nc.vector.tensor_tensor(
                                o_norm[:, par, 64 * half:64 * half + 64].rearrange("p (h d) -> p h d", d=D),
                                bank[7][:, at:at + 64].rearrange("p (h d) -> p h d", d=D),
                                rden[:, par, 8 * half:8 * half + 8].unsqueeze(2).broadcast_to([128, 8, D]), ALU.mult)
                        ins.then_inc(p.o_norm, 1)
                    if g == 1 and real(i - 3, B):
                        dve.wait_ge(p.rstd, 2 * i - 4)
                        nc.vector.tensor_scalar(x_all[:, bass.ts(i - 3, C)], y[:, n, :], mv[:, n, 0:1],
                                                rs[:, n, :], ALU.subtract, ALU.mult).then_inc(p.x, 1)
                    if g == 1 and real(i + 1, B):
                        dve.wait_ge(p.qkv, i + 2)
                        need(dve, p.scores, 4 * i)
                        nc.vector.scalar_tensor_tensor(
                            qg[:, n], bank[6][:, 0:128].unsqueeze(1).broadcast_to([128, UN, 128]), p.bq[:, 0:1],
                            sel_q[:], ALU.add, ALU.mult).then_inc(p.q, 1)
                    if g == 2 and real(i + 1, B):
                        nc.vector.scalar_tensor_tensor(
                            kj[:, n], bank[6][:, 128:256].unsqueeze(1).broadcast_to([128, HU, 128]), p.bk[:, 0:1],
                            sel_k[:], ALU.add, ALU.mult).then_inc(p.k, 1)
                        need(dve, p.pv, 4 * i)
                        nc.vector.tensor_tensor(
                            v_pad[:, n, :].rearrange("p (a b c) -> p a b c", a=2, b=8)[:, :, :, 0:D],
                            bank[6][:, 256:384].rearrange("p (a b c) -> p a b c", a=2, b=8),
                            p.bv[:].rearrange("p (a b c) -> p a b c", a=2, b=8), ALU.add).then_inc(p.v, 1)
                    if g == 3 and real(i - 2, B):
                        dve.wait_ge(p.proj, i - 1)
                        dve.wait_ge(p.res, i - 1)
                        nc.vector.tensor_tensor(y[:, par, :], bank[7][:, 384:512], xb[:, par, :],
                                                ALU.add).then_inc(p.y, 1)
                        dve.wait_ge(p.y, i - 1)
                        nc.vector.bn_stats(st[:, par, :], y[:, par, :])
                        dve.drain()
                        nc.vector.bn_aggr(mv[:, par, :], st[:, par, :]).then_inc(p.mv, 1)

            sequences(dve, step)

        def attention_pool(pool, p):
            if p.before:
                pool.wait_ge(*p.before)

            def step(i, par):
                if real(i + 2, B):
                    need(pool, p.turned, i + 1)
                    if p.cross:
                        nc.gpsimd.tensor_copy(cs[:, par, :], ctx_all[:, bass.ts(i + 2, CTX)])
                    nc.gpsimd.tensor_copy(xs[:, par, :], x_all[:, bass.ts(i + 2, C)]).then_inc(p.copied, 1)
                if real(i - 2, B):
                    need(pool, p.y, i - 3)
                    nc.gpsimd.tensor_tensor(xb[:, par, :], x_all[:, bass.ts(i - 2, C)], p.bo[:],
                                            ALU.add).then_inc(p.res, 1)
                    pool.wait_ge(p.mv, i - 1)
                    nc.gpsimd.tensor_tensor(ve[:, par, :], mv[:, par, 1:2], ln_eps[:, 0:1],
                                            ALU.add).then_inc(p.rstd, 1)
                    pool.wait_ge(p.rstd, 2 * i - 3)
                    nc.gpsimd.tensor_tensor(rs[:, par, :], ve[:, par, :], minus_half[:, 0:1],
                                            ALU.pow).then_inc(p.rstd, 1)

            sequences(pool, step)

        def cols(b):
            return slice(b * 128, (b + 1) * 128)

        def gates_pe(pe, p):
            pe.wait_ge(*p.before)

            def step(i):
                if p.cosine:
                    for h in range(2):
                        pe.wait_ge(p.copied, i + h + 1)
                        need(pe, p.kept, i + h - 1)
                        need(pe, p.chain, i + h - 1)
                        for b in range(GB):
                            nc.tensor.transpose(bank[4 * h][:, cols(b)], xg[:, h, b, :], ident[:])
                        for b in range(GB):
                            last = nc.tensor.transpose(bank[4 * h + 1][0:CTX, cols(b)], cg[:, h, b, :], ident[:])
                        last.then_inc(p.turned, 1)
                    for h in range(2):
                        pe.wait_ge(p.xT, i + h + 1)
                        nc.tensor.matmul(bank[4 * h + 2][0:XH, :], wT[:, 0, 0:XH], xgT[:, h, :],
                                         start=True, stop=True)
                        nc.tensor.matmul(bank[4 * h + 3][0:XH, :], wT[0:CTX, 1, 0:XH], cgT[:, h, :],
                                         start=True, stop=True).then_inc(p.proj, 1)
                    for h in range(2):
                        pe.wait_ge(p.vt, i + h + 1)
                        for b in range(GB):
                            nc.tensor.matmul(bank[4 * h + 1][:, b:b + 1], vT2[:, h, cols(b)], ones[0:XH, 0:1],
                                             start=True, stop=True)
                            nc.tensor.matmul(bank[4 * h + 1][:, GB + b:GB + b + 1], tT2[:, h, cols(b)],
                                             ones[0:XH, 0:1], start=True, stop=True)
                        for b in range(GB):
                            last = nc.tensor.matmul(bank[4 * h][:, cols(b)], vT[:, h, cols(b)], tT[:, h, cols(b)],
                                                    start=True, stop=True)
                        last.then_inc(p.cos, 1)
                    for h in range(2):
                        pe.wait_ge(p.diag, i + h + 1)
                        nc.tensor.matmul(bank[4 * h + 2][:], ones[:], diag[:, h].rearrange("p a b -> p (a b)"),
                                         start=True, stop=True).then_inc(p.R, 1)
                for h in range(2):
                    if p.cosine:
                        pe.wait_ge(p.x1, i + h + 1)
                    else:
                        pe.wait_ge(p.copied, i + h + 1)
                        need(pe, p.kept, i + h - 1)
                        need(pe, p.chain, i + h - 1)
                    for b in range(GB):
                        last = nc.tensor.transpose(bank[4 * h + 3][:, cols(b)], xg[:, h, b, :], ident[:])
                    last.then_inc(p.T1, 1)
                for h in range(2):
                    pe.wait_ge(p.x1T, i + h + 1)
                    for b in range(GB):
                        last = nc.tensor.matmul(bank[4 * h + 1][:, b * p.n:(b + 1) * p.n], xgT[:, h, cols(b)],
                                                p.w[:], start=True, stop=True)
                    last.then_inc(p.logits, 1)

            pairs(pe, step)

        def gates_act(act, p):
            act.wait_ge(*p.before)

            def step(i):
                if p.cosine:
                    for h in range(2):
                        act.wait_ge(p.turned, i + h + 1)
                        nc.scalar.activation(xgT[:, h, :], bank[4 * h][:], ACT.Copy)
                        nc.scalar.activation(cgT[:, h, :], bank[4 * h + 1][0:CTX, :], ACT.Copy).then_inc(p.xT, 1)
                    for h in range(2):
                        act.wait_ge(p.proj, i + h + 1)
                        v, t = bank[4 * h + 2][0:XH, :], bank[4 * h + 3][0:XH, :]
                        nc.scalar.activation(vT2[:, h, :], v, ACT.Square, bias=bvx[:, 0:1])
                        nc.scalar.activation(tT2[:, h, :], t, ACT.Square, bias=btx[:, 0:1])
                        nc.scalar.activation(vT[:, h, :], v, ACT.Identity, bias=bvx[:, 0:1])
                        nc.scalar.activation(tT[:, h, :], t, ACT.Identity, bias=btx[:, 0:1]).then_inc(p.vt, 1)
                for h in range(2):
                    act.wait_ge(p.T1, i + h + 1)
                    need(act, p.logits, i + h - 1)
                    nc.scalar.activation(xgT[:, h, :], bank[4 * h + 3][:], ACT.Copy).then_inc(p.x1T, 1)
                for h in range(2):
                    nc.scalar.activation(in_T[:, bass.ts(i + h, GB * 128)], bank[4 * h + 3][:],
                                         ACT.Copy).then_inc(p.kept, 1)

            pairs(act, step)
            act.wait_ge(p.shifted, 1)
            nc.scalar.activation(pr[:, :, 0:p.n], hot[:, :, 0:p.n], ACT.Exp).then_inc(p.exp, 1)

        def gates_dve(dve, p):
            dve.wait_ge(*p.before)
            n = p.n

            def step(i):
                if p.cosine:
                    for h in range(2):
                        dve.wait_ge(p.cos, i + h + 1)
                        nc.vector.tensor_scalar(nrm[:, h, :], bank[4 * h + 1][:, 0:2 * GB], NORM_FLOOR, None,
                                                ALU.max).then_inc(p.norms, 1)
                    for h in range(2):
                        dve.wait_ge(p.rn, i + h + 1)
                        for b in range(GB):
                            ins = nc.vector.tensor_scalar(diag[:, h, b, :], ident[:], rn[:, h, GB + b:GB + b + 1],
                                                          None, ALU.mult)
                        ins.then_inc(p.diag, 1)
                    for h in range(2):
                        done = 3 * (i + h)
                        dve.wait_ge(p.R, i + h + 1)
                        for b in range(GB):
                            ins = nc.vector.tensor_scalar(cosw[:, h, b, :], bank[4 * h + 2][:, cols(b)],
                                                          rn[:, h, b:b + 1], 1.0 / COS_EPS, ALU.mult, ALU.min)
                        ins.then_inc(p.sum, 1)
                        dve.wait_ge(p.sum, done + 1)
                        nc.vector.tensor_tensor(cosw[:, h], bank[4 * h][:].rearrange("p (a b) -> p a b", a=GB),
                                                cosw[:, h], ALU.mult).then_inc(p.sum, 1)
                        dve.wait_ge(p.sum, done + 2)
                        nc.vector.tensor_tensor(yg[:, h], cosw[:, h], xg[:, h], ALU.add).then_inc(p.sum, 1)
                        dve.wait_ge(p.sum, done + 3)
                        for b in range(GB):
                            nc.vector.bn_stats(gst[:, h, b, :], yg[:, h, b, :])
                        dve.drain()
                        for b in range(GB):
                            ins = nc.vector.bn_aggr(gmv[:, h, b, :], gst[:, h, b, :])
                        ins.then_inc(p.mv, 1)
                    for h in range(2):
                        dve.wait_ge(p.rstd, 2 * (i + h + 1))
                        for b in range(GB):
                            ins = nc.vector.tensor_scalar(xg[:, h, b, :], yg[:, h, b, :], gmv[:, h, b, 0:1],
                                                          grs[:, h, b:b + 1], ALU.subtract, ALU.mult)
                        ins.then_inc(p.x1, 1)
                    for h in range(2):
                        dve.wait_ge(p.x1, i + h + 1)
                        nc.vector.tensor_copy(x_all[:, bass.ts(i + h, GB * C)],
                                              xg[:, h].rearrange("p a b -> p (a b)")).then_inc(p.stored, 1)
                for h in range(2):
                    dve.wait_ge(p.logits, i + h + 1)
                    nc.vector.tensor_copy(logit[:, bass.ts(i + h, GB * n)],
                                          bank[4 * h + 1][:, 0:GB * n]).then_inc(p.chain, 1)

            pairs(dve, step)
            links = [NG]

            def link(ins):
                links[0] += 1
                ins.then_inc(p.chain, 1)
                dve.wait_ge(p.chain, links[0])

            def wide(t):
                return t.unsqueeze(2).broadcast_to([128, B, n])

            def every(t):
                return t.unsqueeze(1).broadcast_to([128, B, n])

            dve.wait_ge(p.chain, NG)
            l = logit[:, 0:B * n].rearrange("p (a b) -> p a b", a=B)
            if p.b is not None:
                link(nc.vector.tensor_tensor(l, l, every(p.b[:]), ALU.add))
            link(nc.vector.reduce_max(sm[:], l, AX))
            nc.vector.tensor_tensor(hot[:, :, 0:n], l, wide(sm[:]), ALU.subtract).then_inc(p.shifted, 1)
            dve.wait_ge(p.exp, 1)
            pn, ln, hn, c1, c2 = (t[:, :, 0:n] for t in (pr, left, hot, coef1, coef2))
            link(nc.vector.reduce_sum(sm[:], pn, AX))
            link(nc.vector.reciprocal(sm2[:], sm[:]))
            link(nc.vector.tensor_tensor(ln, pn, wide(sm2[:]), ALU.mult))
            link(nc.vector.tensor_copy(pn, ln))

            def best(dst):
                link(nc.vector.reduce_max(sm[:], ln, AX))
                link(nc.vector.tensor_tensor(hn, ln, wide(sm[:]), ALU.is_equal))
                link(nc.vector.tensor_tensor(hn, hn, every(p.rank[:]), ALU.mult))
                link(nc.vector.reduce_max(sm2[:], hn, AX))
                link(nc.vector.tensor_tensor(dst, hn, wide(sm2[:]), ALU.is_equal))
                link(nc.vector.scalar_tensor_tensor(ln, dst, -2.0, ln, ALU.mult, ALU.add))

            if p is gates0:
                best(c1)
                link(nc.vector.tensor_copy(g1[:], sm[:]))
                best(c2)
                link(nc.vector.tensor_tensor(c2, c2, pn, ALU.mult))
            else:
                best(c1)
                best(c2)
                link(nc.vector.tensor_tensor(c1, c1, c2, ALU.add))
                best(c2)
                link(nc.vector.tensor_tensor(c1, c1, c2, ALU.add))
                link(nc.vector.tensor_tensor(c1, c1, pn, ALU.mult))
                link(nc.vector.reduce_sum(sm[:], c1, AX))
                link(nc.vector.tensor_scalar(sm[:], sm[:], 1e-12, None, ALU.max))
                link(nc.vector.reciprocal(sm2[:], sm[:]))
                link(nc.vector.tensor_tensor(c1, c1, wide(sm2[:]), ALU.mult))
            p.chained = links[0]

        def gates_pool(pool, p):
            pool.wait_ge(*p.before)

            def step(i):
                for h in range(2):
                    need(pool, p.T1, i + h - 1)
                    if p.cosine:
                        need(pool, p.stored, i + h - 1)
                        nc.gpsimd.tensor_copy(cg[:, h].rearrange("p a b -> p (a b)"),
                                              ctx_all[:, bass.ts(i + h, GB * CTX)])
                    nc.gpsimd.tensor_copy(xg[:, h].rearrange("p a b -> p (a b)"),
                                          x_all[:, bass.ts(i + h, GB * C)]).then_inc(p.copied, 1)
                if p.cosine:
                    for h in range(2):
                        pool.wait_ge(p.norms, i + h + 1)
                        nc.gpsimd.tensor_tensor(rn[:, h, :], nrm[:, h, :], minus_half[:], ALU.pow).then_inc(p.rn, 1)
                    for h in range(2):
                        pool.wait_ge(p.mv, i + h + 1)
                        nc.gpsimd.tensor_tensor(gve[:, h, :], gmv[:, h, :, 1], ln_eps[:], ALU.add).then_inc(p.rstd, 1)
                        pool.wait_ge(p.rstd, 2 * (i + h) + 1)
                        nc.gpsimd.tensor_tensor(grs[:, h, :], gve[:, h, :], minus_half[:, 0:GB],
                                                ALU.pow).then_inc(p.rstd, 1)

            pairs(pool, step)

        def experts_pe(pe, p):
            n = p.n
            pe.wait_ge(p.gates.kept, NG)
            pe.wait_ge(p.gates.chain, NG)
            if p.kind == "fuse":
                pe.wait_ge(boosting.boostTs, NG)

            def turn_boosted(i):
                pe.wait_ge(p.boost, i + 1)
                for b in range(GB):
                    last = nc.tensor.transpose(bank[6][:, cols(b)], total[:, b, :], ident[:])
                last.then_inc(p.boostT, 1)

            def step(i):
                def up(e):
                    k = i * n + e
                    need(pe, p.h, 2 * (k - 1))
                    for c in range(2):
                        nc.tensor.matmul(bank[2 * (e % 2) + c][:], p.w1[:, e, c * 128:(c + 1) * 128],
                                         in_T[:, bass.ts(i, GB * 128)], start=True, stop=True).then_inc(p.up, 1)

                def down(e):
                    k = i * n + e
                    pe.wait_ge(p.h, 2 * (k + 1))
                    need(pe, p.acc, k - 1)
                    for b in range(GB):
                        for c in range(2):
                            last = nc.tensor.matmul(bank[4 + e % 2][:, cols(b)], hid[:, e % 2, c, cols(b)],
                                                    p.w2[:, e, c, :], start=(c == 0), stop=(c == 1))
                    last.then_inc(p.down, 1)

                up(0)
                for e in range(n):
                    if e + 1 < n:
                        up(e + 1)
                    down(e)
                    if e == 2 and p.kind == "boost" and real(i - 1, NG):
                        turn_boosted(i - 1)
                    if e == 4:
                        pe.wait_ge(p.padded, i + 1)
                        if p.kind == "boost":
                            need(pe, p.boostTs, i)
                        for b in range(GB):
                            last = nc.tensor.transpose(bank[6][:, cols(b)], cpad[:, b, :], ident[:])
                        last.then_inc(p.cT, 1)
                    if e == 5:
                        pe.wait_ge(p.cTs, i + 1)
                        need(pe, p.total, i)
                        for b in range(GB):
                            last = nc.tensor.matmul(bank[7][:, cols(b)], cpT[:, b, :], p.b2[:],
                                                    start=True, stop=True)
                        last.then_inc(p.b2s, 1)

            groups(pe, step)
            if p.kind == "boost":
                turn_boosted(NG - 1)

        def experts_act(act, p):
            n = p.n
            act.wait_ge(*p.gates.before)

            def keep_boosted(i):
                act.wait_ge(p.boostT, i + 1)
                nc.scalar.activation(in_T[:, bass.ts(i, GB * 128)], bank[6][:], ACT.Copy).then_inc(p.boostTs, 1)

            def step(i):
                for e in range(n):
                    k = i * n + e
                    need(act, p.down, k - 1)
                    for c in range(2):
                        act.wait_ge(p.up, 2 * k + c + 1)
                        nc.scalar.activation(hid[:, e % 2, c, :], bank[2 * (e % 2) + c][:], ACT.Relu,
                                             bias=p.b1[:, 2 * e + c:2 * e + c + 1]).then_inc(p.h, 1)
                    if e == 3 and p.kind == "boost" and real(i - 1, NG):
                        keep_boosted(i - 1)
                    if e == 5:
                        act.wait_ge(p.cT, i + 1)
                        need(act, p.b2s, i)
                        nc.scalar.activation(cpT[:].rearrange("p a b -> p (a b)"), bank[6][:],
                                             ACT.Copy).then_inc(p.cTs, 1)

            groups(act, step)
            if p.kind == "boost":
                keep_boosted(NG - 1)

        def experts_dve(dve, p):
            n = p.n
            if p.kind == "boost":
                dve.wait_ge(p.gates.stored, NG)
            if p.kind == "fuse":
                dve.wait_ge(boosting.boostT, NG)
            TAIL = 5 if p.kind == "fuse" else 2

            def statistics(src):
                for b in range(GB):
                    nc.vector.bn_stats(gst[:, 0, b, :], src[:, b, :])
                dve.drain()
                for b in range(GB):
                    ins = nc.vector.bn_aggr(gmv[:, 0, b, :], gst[:, 0, b, :])
                ins.then_inc(p.mv, 1)

            def normalise(dst, src, m):
                dve.wait_ge(p.rstd, 2 * m)
                for b in range(GB):
                    ins = nc.vector.tensor_scalar(dst[:, b, :], src[:, b, :], gmv[:, 0, b, 0:1],
                                                  grs[:, 0, b:b + 1], ALU.subtract, ALU.mult)
                return ins

            def every(t):
                return t[:].unsqueeze(1).broadcast_to([128, GB, C])

            def tail(i, part):
                kept = x_all[:, bass.ts(i, GB * C)].rearrange("p (a b) -> p a b", a=GB)
                if p.kind == "boost":
                    if part == 0:
                        need(dve, p.boostT, i)
                        nc.vector.scalar_tensor_tensor(
                            total[:], eo_all[:, bass.ts(i, GB * C)].rearrange("p (a b) -> p a b", a=GB), 0.5, kept,
                            ALU.mult, ALU.add).then_inc(p.boost, 1)
                    return
                if p.kind == "fuse":
                    if part == 0:
                        for b in range(GB):
                            ins = nc.vector.scalar_tensor_tensor(
                                total[:, b, :], eo_all[:, bass.ts(GB * i + b, C)], g1[:, bass.ds(GB * i + b, 1)],
                                total[:, b, :], ALU.mult, ALU.add)
                        ins.then_inc(p.tail, 1)
                        dve.wait_ge(p.tail, TAIL * i + 1)
                        nc.vector.tensor_tensor(total[:], total[:], kept, ALU.add).then_inc(p.tail, 1)
                    if part == 1:
                        dve.wait_ge(p.tail, TAIL * i + 2)
                        statistics(total)
                    if part == 2:
                        normalise(norm1, total, 2 * i + 1).then_inc(p.tail, 1)
                        dve.wait_ge(p.tail, TAIL * i + 3)
                        nc.vector.tensor_tensor(norm1[:], norm1[:], every(gamma), ALU.mult).then_inc(p.tail, 1)
                    if part == 3:
                        dve.wait_ge(p.tail, TAIL * i + 4)
                        nc.vector.tensor_tensor(norm1[:], norm1[:], every(beta), ALU.add).then_inc(p.tail, 1)
                        dve.wait_ge(p.tail, TAIL * i + 5)
                        nc.vector.tensor_tensor(total[:], norm1[:], kept, ALU.add).then_inc(p.boost, 1)
                    if part == 4:
                        dve.wait_ge(p.boost, i + 1)
                        statistics(total)
                    if part == 5:
                        normalise(kept, total, 2 * i + 2).then_inc(p.x, 1)
                    return
                if part == 0:
                    nc.vector.tensor_tensor(total[:], total[:], kept, ALU.add).then_inc(p.tail, 1)
                if part == 1:
                    dve.wait_ge(p.tail, i + 1)
                    statistics(total)
                if part == 2:
                    need(dve, p.out, 16 * i)
                    normalise(xo, total, i + 1).then_inc(p.x, 1)

            def step(i):
                for e in range(n):
                    k = i * n + e
                    dve.wait_ge(p.down, k + 1)
                    need(dve, p.acc, k)
                    for b in range(GB):
                        o = bank[4 + e % 2][:, cols(b)]
                        gate = p.coef[:].rearrange("p a b -> p (a b)")[:, bass.ds((GB * i + b) * E1 + e, 1)]
                        if e == 0:
                            ins = nc.vector.tensor_scalar(acc[:, b, :], o, gate, None, ALU.mult)
                        else:
                            ins = nc.vector.scalar_tensor_tensor(acc[:, b, :], o, gate, acc[:, b, :],
                                                                 ALU.mult, ALU.add)
                    ins.then_inc(p.acc, 1)
                    if e < 6 and real(i - 1, NG):
                        tail(i - 1, e)
                dve.wait_ge(p.b2s, i + 1)
                dve.wait_ge(p.acc, (i + 1) * n)
                bias = bank[7][:].rearrange("p (a b) -> p a b", a=GB)
                dst = eo_all[:, bass.ts(i, GB * C)].rearrange("p (a b) -> p a b", a=GB) if p.kind == "boost" \
                    else total[:]
                if p.kind != "boost":
                    need(dve, p.x, i)
                nc.vector.tensor_tensor(dst, bias, acc[:], ALU.add).then_inc(p.total, 1)
                dve.wait_ge(p.total, i + 1)

            groups(dve, step)
            for part in range(6):
                tail(NG - 1, part)

        def experts_pool(pool, p):
            n = p.n
            pool.wait_ge(p.gates.chain, p.gates.chained)
            if p.kind == "fuse":
                pool.wait_ge(boosting.cT, NG)
            per_group = {"boost": 0, "fuse": 2, "mix": 1}[p.kind]

            def norms(i):
                for k in range(per_group):
                    m = per_group * i + k + 1
                    pool.wait_ge(p.mv, m)
                    nc.gpsimd.tensor_tensor(gve[:, 0, :], gmv[:, 0, :, 1], ln_eps[:], ALU.add).then_inc(p.rstd, 1)
                    pool.wait_ge(p.rstd, 2 * m - 1)
                    nc.gpsimd.tensor_tensor(grs[:, 0, :], gve[:, 0, :], minus_half[:, 0:GB],
                                            ALU.pow).then_inc(p.rstd, 1)

            def step(i):
                need(pool, p.cT, i)
                flat = p.coef[:].rearrange("p a b -> p (a b)")[:, bass.ts(i, GB * E1)]
                nc.gpsimd.tensor_copy(cpad[:, :, 0:n],
                                      flat.rearrange("p (a b) -> p a b", a=GB)[:, :, 0:n]).then_inc(p.padded, 1)
                if real(i - 1, NG):
                    norms(i - 1)

            groups(pool, step)
            norms(NG - 1)

        block = ctx.enter_context(nc.Block())

        @block.sync
        def _(sp):
            for dst, src in small_in:
                sp.dma_start(dst, src).then_inc(s_in, 16)
            def step(i):
                sp.wait_ge(mixing.x, i + 1)
                sp.dma_start(out[bass.ts(i, GB), :, :].rearrange("b p c -> p b c"), xo[:]).then_inc(mixing.out, 16)

            groups(sp, step)
            sp.wait_ge(mixing.out, 16 * NG)

        @block.tensor
        def _(pe):
            pe.wait_ge(s_in, 16 * len(small_in))
            pe.wait_ge(s_const, CONSTS)
            for k, (rows, cols) in enumerate(TURNED):
                last = nc.tensor.transpose(bank[k // 3][0:cols, (k % 3) * 128:(k % 3) * 128 + rows],
                                           raw[0:rows, k, 0:cols], ident[0:rows, 0:rows])
            last.then_inc(s_rawT, 1)
            pe.wait_ge(s_wT, 1)
            attention_pe(pe, first)
            pe.wait_ge(s_w, LATE)
            pe.wait_ge(s_b2, 16 * len(padded_in))
            gates_pe(pe, gates0)
            experts_pe(pe, boosting)
            experts_pe(pe, fusing)
            attention_pe(pe, second)
            attention_pe(pe, third)
            gates_pe(pe, gates1)
            experts_pe(pe, mixing)

        @block.scalar
        def _(act):
            for dst, src in late_in:
                act.dma_start(dst, src).then_inc(s_w, 16)
            act.wait_ge(s_rawT, 1)
            for k, (rows, cols) in enumerate(TURNED):
                last = nc.scalar.activation(wT[0:cols, k, 0:rows],
                                            bank[k // 3][0:cols, (k % 3) * 128:(k % 3) * 128 + rows], ACT.Copy)
            last.then_inc(s_wT, 1)
            attention_act(act, first)
            act.wait_ge(s_w, LATE)
            gates_act(act, gates0)
            experts_act(act, boosting)
            experts_act(act, fusing)
            attention_act(act, second)
            attention_act(act, third)
            gates_act(act, gates1)
            experts_act(act, mixing)

        @block.vector
        def _(dve):
            nc.vector.memset(v_pad[:].rearrange("p a b -> p (a b)"), 0.0).then_inc(s_const, 1)
            nc.vector.memset(ones[:], 1.0).then_inc(s_const, 1)
            nc.vector.memset(minus_half[:], -0.5).then_inc(s_const, 1)
            nc.vector.memset(zero_col[:], 0.0).then_inc(s_const, 1)
            nc.vector.memset(zero_row[:], 0.0).then_inc(s_const, 1)
            nc.vector.memset(cpad[:], 0.0).then_inc(s_const, 1)
            nc.vector.memset(ln_eps[:], LN_EPS).then_inc(s_const, 1)
            dve.wait_ge(s_const, 7)
            for par in range(2):
                for half in range(2):
                    at = 64 if half == 0 else 1024
                    nc.vector.memset(v_pad[:, par, at:at + HALF].rearrange("p (b c) -> p b c", c=136)[:, :, 0:D],
                                     1.0).then_inc(s_const, 1)
            dve.wait_ge(s_in, 16 * len(small_in))
            nc.vector.tensor_copy(sel_q[:], sel[:, 0, :].unsqueeze(2).broadcast_to([128, UN, 128]))
            nc.vector.tensor_copy(sel_k[:], sel[:, 1, :].unsqueeze(2).broadcast_to([128, HU, 128])).then_inc(s_const, 1)
            dve.wait_ge(s_const, CONSTS)
            attention_dve(dve, first)
            dve.wait_ge(s_w, LATE)
            gates_dve(dve, gates0)
            experts_dve(dve, boosting)
            experts_dve(dve, fusing)
            attention_dve(dve, second)
            attention_dve(dve, third)
            gates_dve(dve, gates1)
            experts_dve(dve, mixing)

        @block.gpsimd
        def _(pool):
            nc.gpsimd.memset(b2_0[:], 0.0).then_inc(s_zeroed, 1)
            nc.gpsimd.memset(b2_1[:], 0.0).then_inc(s_zeroed, 1)
            pool.wait_ge(s_zeroed, 2)
            for dst, src in padded_in:
                pool.dma_start(dst, src).then_inc(s_b2, 16)
            pool.wait_ge(s_const, CONSTS)
            pool.wait_ge(s_in, 16 * len(small_in))
            attention_pool(pool, first)
            pool.wait_ge(s_w, LATE)
            gates_pool(pool, gates0)
            experts_pool(pool, boosting)
            experts_pool(pool, fusing)
            attention_pool(pool, second)
            attention_pool(pool, third)
            gates_pool(pool, gates1)
            experts_pool(pool, mixing)


_INS = ['x', 'ctx_768', 'L0_attn_w_qkv', 'L0_attn_b_qkv', 'L0_attn_w_out', 'L0_attn_b_out', 'L0_xattn_Wv',
        'L0_xattn_bv', 'L0_xattn_Wt', 'L0_xattn_bt', 'L0_ffn_gate_W', 'L0_ffn_gate_b', 'L0_ffn_W1', 'L0_ffn_b1',
        'L0_ffn_W2', 'L0_ffn_b2', 'L0_ffn_ln_gamma', 'L0_ffn_ln_beta', 'L1_attn_Wq', 'L1_attn_Wk', 'L1_attn_Wv',
        'L1_attn_Wo', 'L1_xattn_wq', 'L1_xattn_bq', 'L1_xattn_wk', 'L1_xattn_bk', 'L1_xattn_wv', 'L1_xattn_bv',
        'L1_xattn_wo', 'L1_xattn_bo', 'L1_ffn_gate', 'L1_ffn_W1', 'L1_ffn_b1', 'L1_ffn_W2', 'L1_ffn_b2']


def constants():
    p = np.arange(128)
    sel = np.zeros((128, 2, UN), np.float32)
    sel[:, 0, :] = (p[:, None] // (HU * D) == np.arange(UN)) * np.float32(D ** -0.5)
    sel[:, 1, :] = p[:, None] // D % HU == np.arange(HU)
    return {
        "ident": np.eye(128, dtype=np.float32),
        "causal": np.where(p[:, None] >= p[None, :], 0.0, -BIG).astype(np.float32),
        "sel": sel,
        "rank0": np.arange(E0, 0, -1).astype(np.float32),
        "rank1": np.arange(E1, 0, -1).astype(np.float32),
    }


def kernel(**inputs):
    import concourse.bacc as _bacc
    from concourse.bass_utils import run_bass_kernel_spmd as _run

    nc = _bacc.Bacc("TRN2", target_bir_lowering=False, num_devices=1)
    arrays, aps = {}, {}
    given = {name: np.ascontiguousarray(inputs[name]) for name in _INS}
    for name, v in {**given, **constants()}.items():
        arrays[f"in_{name}"] = v
        aps[name] = nc.dram_tensor(f"in_{name}", v.shape, mybir.dt.from_np(v.dtype), kind="ExternalInput").ap()
    out = nc.dram_tensor("out_0", (B, T, C), F32, kind="ExternalOutput").ap()
    decoder(nc, aps, out)
    r = _run(nc, [arrays], core_ids=[0])
    return r.results[0]["out_0"]
```

```python
import numpy as np
import concourse.bass as bass
from concourse import mybir
from contextlib import ExitStack

B, T, C, H = 16, 128, 128, 16
D = C // H
CTX = 96
XH = 64
FH = 256
E0, E1 = 8, 16
GB = 4
NG = B // GB
HU = 4
UN = H // HU
LN_EPS = 1e-5
COS_EPS = 1e-8
NORM_FLOOR = 1e-30
BIG = 1e30

F32 = mybir.dt.float32
F32R = mybir.dt.float32r
ALU = mybir.AluOpType
ACT = mybir.ActivationFunctionType
AX = mybir.AxisListType.X


def need(eng, sem, value):
    if isinstance(value, int) and value <= 0:
        return
    eng.wait_ge(sem, value)


def real(b, n):
    return not isinstance(b, int) or 0 <= b < n


def decoder(nc, a, out):
    ctx = ExitStack()
    with ctx:
        def sb(name, shape, dt=F32):
            return ctx.enter_context(nc.sbuf_tensor(name, shape, dt))

        def sem(name):
            return ctx.enter_context(nc.semaphore(name))

        bank = [ctx.enter_context(nc.psum_tensor(f"bank{n}", [128, 512], F32)) for n in range(8)]

        x_all = sb("x_all", [128, B * C])
        ctx_all = sb("ctx_all", [128, B * CTX])
        ident = sb("ident", [128, 128])
        causal = sb("causal", [128, 128])
        ident_r = sb("ident_r", [128, 128], F32R)
        causal_r = sb("causal_r", [128, 128], F32R)
        sel = sb("sel", [128, 2, UN])
        sel_q = sb("sel_q", [128, UN, 128])
        sel_k = sb("sel_k", [128, HU, 128])
        ones = sb("ones", [128, 128])
        sum_halves = sb("sum_halves", [128, 128])
        minus_half = sb("minus_half", [128, GB, 2])
        ln_eps = sb("ln_eps", [128, GB])
        zero_col = sb("zero_col", [128, 1])
        zero_row = sb("zero_row", [128, 128])

        w_qkv = sb("w_qkv", [128, 3 * C])
        bq0 = sb("bq0", [128, 1])
        bk0 = sb("bk0", [128, 1])
        bv0 = sb("bv0", [128, C])
        w_out0 = sb("w_out0", [128, C])
        bo0 = sb("bo0", [128, C])

        raw = sb("raw", [128, 8, 128])
        wT = sb("wT", [128, 8, 128])
        b1_0 = wT[:, 6, 0:2 * E0]
        b1_1 = wT[:, 7, 0:2 * E1]
        wv_cos = sb("wv_cos", [128, 128])
        wt_cos = sb("wt_cos", [CTX, 128])
        bvx = sb("bvx", [128, 1])
        btx = sb("btx", [128, 1])

        wqx = sb("wqx", [128, C])
        wkx = sb("wkx", [CTX, C])
        wvx = sb("wvx", [CTX, C])
        wox = sb("wox", [128, C])
        bq1 = sb("bq1", [128, 1])
        bk1 = sb("bk1", [128, 1])
        bv1 = sb("bv1", [128, C])
        bo1 = sb("bo1", [128, C])

        gate_w0 = sb("gate_w0", [128, 128])
        gate_b0 = sb("gate_b0", [128, E0])
        gate_w1 = sb("gate_w1", [128, 128])
        gamma = sb("gamma", [128, C])
        beta = sb("beta", [128, C])
        w1_hi = sb("w1_hi", [128, (E0 + E1) * FH], F32R)
        w1_lo = sb("w1_lo", [128, (E0 + E1) * FH], F32R)
        w2_0 = sb("w2_0", [128, E0, 2, C])
        w2_1 = sb("w2_1", [128, E1, 2, C])
        b2_0 = sb("b2_0", [128, C])
        b2_1 = sb("b2_1", [128, C])
        rank0 = sb("rank0", [128, E0])
        rank1 = sb("rank1", [128, E1])

        xs = sb("xs", [128, 2, C])
        cs = sb("cs", [128, 2, CTX])
        xT = sb("xT", [128, 2, 128])
        cT = sb("cT", [CTX, 2, 128])
        qg = sb("qg", [128, 2, UN, 128])
        kj = sb("kj", [128, 2, HU, 128])
        v_f32 = sb("v_f32", [128, 2, C])
        WIN = 128 + 16
        v_pad = sb("v_pad", [128, 2, 2, 4 * WIN], F32R)
        neg_max = sb("neg_max", [128, UN, HU])
        probs = sb("probs", [128, 4, HU, 128])
        probsT_hi = sb("probsT_hi", [128, 2, HU, 128], F32R)
        probsT_lo = sb("probsT_lo", [128, 2, HU, 128], F32R)
        o_raw = sb("o_raw", [128, 2, 256])
        den = sb("den", [128, 2, H])
        rden = sb("rden", [128, 2, H])
        o_norm = sb("o_norm", [128, 2, C])
        oT = sb("oT", [128, 2, 128])
        xb = sb("xb", [128, 2, C])
        y = sb("y", [128, 2, C])
        st = sb("st", [128, 2, 6])
        mv = sb("mv", [128, 2, 2])
        ve = sb("ve", [128, 2, 1])
        rs = sb("rs", [128, 2, 1])

        xgT = qg[:].rearrange("p h b c -> p h (b c)")
        x1T = sb("x1T", [128, 2, GB * 128])
        cgT = kj[0:CTX].rearrange("p h b c -> p h (b c)")
        yg = sb("yg", [128, 2, GB, C])
        w1_raw = sb("w1_raw", [128, (E0 + E1) * FH])
        cosine_T = w1_raw[:, 0:4096].rearrange("p (k h c) -> p k h c", k=4, h=2)
        vT, tT, sq = (cosine_T[:, k] for k in range(3))
        diag = w1_raw[:, 4096:5120].rearrange("p (h b c) -> p h b c", h=2, b=GB)
        cosw = w1_raw[:, 5120:6144].rearrange("p (h b c) -> p h b c", h=2, b=GB)
        nrm = sb("nrm", [128, 2, GB, 2])
        rn = sb("rn", [128, 2, GB, 2])
        gst = sb("gst", [128, 2, GB, 6])
        gmv = sb("gmv", [128, 2, GB, 2])
        gve = sb("gve", [128, 2, GB])
        grs = sb("grs", [128, 2, GB])
        in_hi = sb("in_hi", [128, B * 128], F32R)
        in_lo = sb("in_lo", [128, B * 128], F32R)
        eo_all = cosine_T[:, 0:2].rearrange("p a b c -> p (a b c)")
        logit, pr = (o_raw[:, k].rearrange("p (b e) -> p b e", e=E1) for k in range(2))
        choice = w1_raw[:, 3072:4096].rearrange("p (k b e) -> p k b e", k=4, e=E1)
        left, hot, coef1, coef2 = (choice[:, k] for k in range(4))
        sm = sb("sm", [128, B])
        sm2 = sb("sm2", [128, B])
        g1 = sb("g1", [128, B])
        hid = probs[:].rearrange("p (a b) c d -> p a b (c d)", a=2)
        acc = w1_raw[:, 2048:2560].rearrange("p (b c) -> p b c", b=GB)
        cpad = sb("cpad", [128, GB, 128])
        cpT = w1_raw[:, 4096:4608].rearrange("p (b c) -> p b c", b=GB)
        total = w1_raw[:, 2560:3072].rearrange("p (b c) -> p b c", b=GB)
        norm1 = raw[:, 0:4, :]
        xo = raw[:, 4:8, :]

        s_first = sem("s_first")
        s_tokens = sem("s_tokens")
        s_w1 = sem("s_w1")
        s_split = sem("s_split")
        s_late = sem("s_late")
        s_const = sem("s_const")
        s_rawT = sem("s_rawT")
        s_wT = sem("s_wT")

        def column(v):
            return v.rearrange("(c o) -> c o", o=1)

        def rows(v):
            return v.partition_broadcast(128)

        x_view = x_all[:].rearrange("p (b c) -> p b c", b=B)
        x_rows = a["x"].rearrange("b p c -> p b c")
        first_sp = [(x_view[:, 0:GB], x_rows[:, 0:GB]), (ident[:], a["ident"]), (causal[:], a["causal"]),
                    (bv0[:], rows(a["L0_attn_b_qkv"][2 * C:3 * C])), (w_out0[:], a["L0_attn_w_out"])]
        first_act = [(w_qkv[:], a["L0_attn_w_qkv"]), (sel[:], a["sel"]), (bq0[:], column(a["L0_attn_b_qkv"][0:C])),
                     (bk0[:], column(a["L0_attn_b_qkv"][C:2 * C])), (bo0[:], rows(a["L0_attn_b_out"]))]
        FIRST = 16 * (len(first_sp) + len(first_act))
        tokens_sp = [(x_view[:, g:g + GB], x_rows[:, g:g + GB]) for g in range(GB, B, GB)]
        TOKENS = 16 * len(tokens_sp)
        w1_view = w1_raw[:].rearrange("p (e h) -> p e h", e=E0 + E1)
        w1_act = [(w1_view[:, 0:E0], a["L0_ffn_W1"].rearrange("e c h -> c e h")),
                  (w1_view[:, E0:E0 + E1], a["L1_ffn_W1"].rearrange("e c h -> c e h"))]
        late_sp = [(raw[0:XH, 0, :], a["L0_xattn_Wv"]), (raw[0:XH, 1, 0:CTX], a["L0_xattn_Wt"]),
                   (raw[:, 2, :], a["L1_attn_Wq"]), (raw[:, 3, :], a["L1_attn_Wk"]),
                   (raw[:, 4, :], a["L1_attn_Wv"]), (raw[:, 5, :], a["L1_attn_Wo"]),
                   (raw[0:2 * E0, 6, :], a["L0_ffn_b1"].rearrange("e (k h) -> (e k) h", k=2)),
                   (raw[0:2 * E1, 7, :], a["L1_ffn_b1"].rearrange("e (k h) -> (e k) h", k=2)),
                   (ctx_all[:].rearrange("p (b c) -> p b c", b=B), a["ctx_768"].rearrange("b p c -> p b c")),
                   (bvx[0:XH], column(a["L0_xattn_bv"])),
                   (btx[0:XH], column(a["L0_xattn_bt"])), (btx[XH:128], column(a["L0_xattn_bt"])),
                   (gate_w0[:, 0:E0], a["L0_ffn_gate_W"]), (gate_b0[:], rows(a["L0_ffn_gate_b"])),
                   (rank0[:], rows(a["rank0"])), (gate_w1[:, 0:E1], a["L1_ffn_gate"]), (rank1[:], rows(a["rank1"])),
                   (b2_0[0:E0, :], a["L0_ffn_b2"]), (b2_1[0:E1, :], a["L1_ffn_b2"]),
                   (gamma[:], rows(a["L0_ffn_ln_gamma"])), (beta[:], rows(a["L0_ffn_ln_beta"])),
                   (wqx[:], a["L1_xattn_wq"]), (wkx[:], a["L1_xattn_wk"]),
                   (wvx[:], a["L1_xattn_wv"]), (wox[:], a["L1_xattn_wo"]),
                   (bq1[:], column(a["L1_xattn_bq"])), (bk1[:], column(a["L1_xattn_bk"])),
                   (bv1[:], rows(a["L1_xattn_bv"])), (bo1[:], rows(a["L1_xattn_bo"])),
                   (w2_0[:], a["L0_ffn_W2"].rearrange("e (k h) c -> h e k c", k=2)),
                   (w2_1[:], a["L1_ffn_W2"].rearrange("e (k h) c -> h e k c", k=2))]
        LATE = 16 * len(late_sp)
        CONSTS = 14

        class Layer:

            def __init__(self, wq, wk, wv, wo, bq, bk, bv, bo, causal, cross):
                self.wq, self.wk, self.wv, self.wo, self.bq = wq, wk, wv, wo, bq
                self.bk, self.bv, self.bo, self.causal, self.cross = bk, bv, bo, causal, cross

        class Attention:

            def __init__(self, name, layers, before):
                self.layers, self.before = layers, before
                self.n = B * len(layers)
                self.copied = sem(name + "_copied")
                self.turned = sem(name + "_turned")
                self.xT = sem(name + "_xT")
                self.qkv = sem(name + "_qkv")
                self.qk = sem(name + "_qk")
                self.v = sem(name + "_v")
                self.v_lo = sem(name + "_v_lo")
                self.scores = sem(name + "_scores")
                self.max = sem(name + "_max")
                self.exp = sem(name + "_exp")
                self.pT = sem(name + "_pT")
                self.probsT = sem(name + "_probsT")
                self.low = sem(name + "_low")
                self.pv = sem(name + "_pv")
                self.o_raw = sem(name + "_o_raw")
                self.o_tok = sem(name + "_o_tok")
                self.rden = sem(name + "_rden")
                self.o_norm = sem(name + "_o_norm")
                self.o_back = sem(name + "_o_back")
                self.oT = sem(name + "_oT")
                self.proj = sem(name + "_proj")
                self.res = sem(name + "_res")
                self.y = sem(name + "_y")
                self.mv = sem(name + "_mv")
                self.rstd = sem(name + "_rstd")
                self.x = sem(name + "_x")

        class Gates:

            def __init__(self, name, n, w, b, rank, cosine, before):
                self.n, self.w, self.b, self.rank, self.cosine = n, w, b, rank, cosine
                self.before, self.y = (before.x, before.n), before.y
                self.turned = sem(name + "_turned") if cosine else None
                self.xT = sem(name + "_xT") if cosine else None
                self.proj = sem(name + "_proj") if cosine else None
                self.vt = sem(name + "_vt") if cosine else None
                self.cos = sem(name + "_cos") if cosine else None
                self.norms = sem(name + "_norms") if cosine else None
                self.rn = sem(name + "_rn") if cosine else None
                self.diag = sem(name + "_diag") if cosine else None
                self.R = sem(name + "_R") if cosine else None
                self.sum = sem(name + "_sum") if cosine else None
                self.mv = sem(name + "_mv") if cosine else None
                self.rstd = sem(name + "_rstd") if cosine else None
                self.x1 = sem(name + "_x1") if cosine else None
                self.T1 = sem(name + "_T1")
                self.x1T = sem(name + "_x1T")
                self.logits = sem(name + "_logits")
                self.kept = sem(name + "_kept")
                self.low = sem(name + "_low")
                self.exp = sem(name + "_exp")
                self.chain = sem(name + "_chain")
                self.shifts = 2 if b is None else 3

        class Round:

            def __init__(self, name, gates, first, w2, b1, b2, coef, kind):
                self.gates, self.n, self.coef, self.kind = gates, gates.n, coef, kind
                self.first, self.w2, self.b1, self.b2 = first, w2, b1, b2
                self.up = sem(name + "_up")
                self.h = sem(name + "_h")
                self.down = sem(name + "_down")
                self.acc = sem(name + "_acc")
                self.padded = sem(name + "_padded")
                self.cT = sem(name + "_cT")
                self.cTs = sem(name + "_cTs")
                self.b2s = sem(name + "_b2s")
                self.total = sem(name + "_total")
                self.boost = sem(name + "_boost") if kind != "mix" else None
                self.boostT = sem(name + "_boostT") if kind == "boost" else None
                self.boost_lo = sem(name + "_boost_lo") if kind == "boost" else None
                self.boostTs = sem(name + "_boostTs") if kind == "boost" else None
                self.tail = sem(name + "_tail") if kind != "boost" else None
                self.mv = sem(name + "_mv") if kind != "boost" else None
                self.rstd = sem(name + "_rstd") if kind != "boost" else None
                self.x = sem(name + "_x") if kind != "boost" else None
                self.out = sem(name + "_out") if kind == "mix" else None

        first = Attention("a0", [Layer(w_qkv[:, 0:C], w_qkv[:, C:2 * C], w_qkv[:, 2 * C:3 * C], w_out0[:],
                                       bq0, bk0, bv0, bo0, True, False)], None)
        gates0 = Gates("g0", E0, gate_w0, gate_b0, rank0, True, first)
        boosting = Round("r0", gates0, 0, w2_0, b1_0, b2_0, coef1, "boost")
        fusing = Round("r1", gates0, 0, w2_0, b1_0, b2_0, coef2, "fuse")
        later = Attention("a1", [Layer(wT[:, 2, :], wT[:, 3, :], wT[:, 4, :], wT[:, 5, :],
                                       zero_col, zero_col, zero_row, zero_row, True, False),
                                 Layer(wqx[:], wkx[:], wvx[:], wox[:], bq1, bk1, bv1, bo1, False, True)],
                          (fusing.total, NG))
        gates1 = Gates("g1", E1, gate_w1, None, rank1, False, later)
        mixing = Round("r2", gates1, E0, w2_1, b1_1, b2_1, coef1, "mix")

        def sequences(eng, p, step):
            for i in range(-2, 4):
                step(i, i % 2, 0)
            for l in range(len(p.layers)):
                with eng.Fori(B * l + 4, B * l + B - 3, 2) as i:
                    step(i, 0, l)
                    step(i + 1, 1, l)
                last = l + 1 == len(p.layers)
                for i in range(B * l + B - 2, B * l + B + (3 if last else 4)):
                    step(i, i % 2, l)

        def place(p, i, l):
            l = i // B if isinstance(i, int) else l
            return p.layers[l], i - B * l

        def pairs(eng, step):
            for i in range(0, NG, 2):
                step(i)

        def groups(eng, step):
            step(0)
            with eng.Fori(1, NG, 1) as i:
                step(i)

        def slot(g, n):
            return g % n

        def attention_pe(pe, p):
            if p.before:
                pe.wait_ge(*p.before)

            def scores(i, g, par, l):
                layer, _ = place(p, i, l)
                u = 4 * i + g
                if g == 0:
                    need(pe, p.qk, i + 1)
                need(pe, p.exp, u - 1)
                if layer.causal:
                    nc.tensor.matmul(bank[slot(g, 2)][:], ident_r[:],
                                     causal_r[:].unsqueeze(1).broadcast_to([128, HU, 128]), start=True, stop=False)
                nc.tensor.matmul(bank[slot(g, 2)][:], qg[:, par, g, :], kj[:, par].rearrange("p a b -> p (a b)"),
                                 start=not layer.causal, stop=True).then_inc(p.scores, 1)

            def turn(u, g):
                pe.wait_ge(p.exp, u + 1)
                need(pe, p.low, u - 1)
                for j in range(HU):
                    last = nc.tensor.transpose(bank[2 + slot(g, 2)][:, j * 128:(j + 1) * 128],
                                               probs[:, g, j, :], ident[:])
                last.then_inc(p.pT, 1)

            def values(u, i, g, par):
                pe.wait_ge(p.probsT, u + 1)
                if g == 0:
                    pe.wait_ge(p.v_lo, i + 1)
                    need(pe, p.o_raw, i - 1)
                half = g // 2
                for part in (probsT_hi, probsT_lo):
                    if part is probsT_lo:
                        pe.wait_ge(p.low, u + 1)
                    for k in range(2):
                        w = 2 * (g % 2) + k
                        last = nc.tensor.matmul(bank[4 + par][:, half * 256:(half + 1) * 256],
                                                v_pad[:, par, half, 128 * w:128 * w + 128],
                                                part[:, slot(g, 2), 2 * k:2 * k + 2, :].rearrange("p a b -> p (a b)"),
                                                start=(w == 0 and part is probsT_hi),
                                                stop=(w == 3 and part is probsT_lo))
                last.then_inc(p.pv, 1)

            def step(i, par, l):
                n = 1 - par
                for g in range(UN):
                    b2, g2 = (i, g - 2) if g >= 2 else (i - 1, g + 2)
                    if real(b2, p.n):
                        turn(4 * i + g - 2, g2)
                    if real(i, p.n):
                        scores(i, g, par, l)
                    if g == 0:
                        if p is first and isinstance(i, int) and i == B + 1:
                            turn_weights(pe)
                        if real(i + 1, p.n):
                            layer, _ = place(p, i + 1, l)
                            need(pe, p.copied, i + 2)
                            need(pe, p.v, i + 1)
                            last = nc.tensor.transpose(bank[6][:, 384:512], xs[:, n, :], ident[:])
                            if layer.cross:
                                last = nc.tensor.transpose(bank[6][0:CTX, 256:384], cs[:, n, :], ident[:])
                            last.then_inc(p.turned, 1)
                    if g == 1:
                        if real(i + 1, p.n):
                            need(pe, p.xT, i + 2)
                            layer, _ = place(p, i + 1, l)
                            src = cT[:, n, :] if layer.cross else xT[:, n, :]
                            nc.tensor.matmul(bank[6][:, 0:128], layer.wq, xT[:, n, :], start=True, stop=True)
                            nc.tensor.matmul(bank[6][:, 128:256], layer.wk, src, start=True, stop=True)
                            nc.tensor.matmul(bank[6][:, 256:384], src, layer.wv, start=True,
                                             stop=True).then_inc(p.qkv, 1)
                    if g == 3 and real(i - 2, p.n):
                        pe.wait_ge(p.oT, i - 1)
                        layer, _ = place(p, i - 2, l)
                        nc.tensor.matmul(bank[7][:, 384:512], oT[:, par, :], layer.wo,
                                         start=True, stop=True).then_inc(p.proj, 1)
                    b3, g3 = (i, g - 3) if g >= 3 else (i - 1, g + 1)
                    if real(b3, p.n):
                        values(4 * i + g - 3, b3, g3, par if g >= 3 else n)
                    if g == 0 and real(i - 2, p.n):
                        pe.wait_ge(p.o_raw, i - 1)
                        need(pe, p.y, i - 2)
                        for half in range(2):
                            last = nc.tensor.transpose(bank[7][:, half * 128:(half + 1) * 128],
                                                       o_raw[:, par, half * 128:(half + 1) * 128], ident[:])
                        last.then_inc(p.o_tok, 1)
                    if g == 1 and real(i - 2, p.n):
                        pe.wait_ge(p.o_norm, 2 * i - 2)
                        nc.tensor.transpose(bank[7][:, 256:384], o_norm[:, par, :],
                                            ident[:]).then_inc(p.o_back, 1)

            sequences(pe, p, step)

        TURNED = ((XH, C), (XH, CTX), (C, C), (C, C), (C, C), (C, C), (2 * E0, 128), (2 * E1, 128))

        def turned(k):
            rows, cols = TURNED[k]
            return bank[k // 4][0:cols, (k % 4) * 128:(k % 4) * 128 + rows]

        def turn_weights(pe):
            pe.wait_ge(s_late, LATE)
            pe.wait_ge(first.exp, UN * B)
            for k, (rows, cols) in enumerate(TURNED):
                last = nc.tensor.transpose(turned(k), raw[0:rows, k, 0:cols], ident[0:rows, 0:rows])
            last.then_inc(s_rawT, 1)

        def keep_weights(act):
            act.wait_ge(s_rawT, 1)
            for k, (rows, cols) in enumerate(TURNED):
                places = {0: [wv_cos[:, 0:XH]], 1: [wt_cos[:, 0:XH], wt_cos[:, XH:128]]}
                for dst in places.get(k, [wT[0:cols, k, 0:rows]]):
                    last = nc.scalar.activation(dst, turned(k), ACT.Copy)
            last.then_inc(s_wT, 1)

        def attention_act(act, p):
            if p.before:
                act.wait_ge(*p.before)

            def step(i, par, l):
                n = 1 - par
                for g in range(UN):
                    if g == 3 and p is first and isinstance(i, int) and i == B + 1:
                        keep_weights(act)
                    if g == 0 and real(i + 1, p.n):
                        layer, _ = place(p, i + 1, l)
                        act.wait_ge(p.turned, i + 2)
                        need(act, p.qkv, i)
                        if layer.cross:
                            nc.scalar.activation(cT[:, n, :], bank[6][0:CTX, 256:384], ACT.Copy)
                        nc.scalar.activation(xT[:, n, :], bank[6][:, 384:512], ACT.Copy).then_inc(p.xT, 1)
                    b2, g2 = (i, g - 2) if g >= 2 else (i - 1, g + 2)
                    if real(b2, p.n):
                        u = 4 * i + g - 2
                        act.wait_ge(p.pT, u + 1)
                        need(act, p.pv, u - 1)
                        nc.scalar.activation(probsT_hi[:, slot(g2, 2)].rearrange("p a b -> p (a b)"),
                                             bank[2 + slot(g2, 2)][:], ACT.Copy).then_inc(p.probsT, 1)
                    if g == 2 and real(i - 2, p.n):
                        act.wait_ge(p.o_back, i - 1)
                        need(act, p.proj, i - 3)
                        nc.scalar.activation(oT[:, par, :], bank[7][:, 256:384], ACT.Copy).then_inc(p.oT, 1)
                    if g == 3 and real(i - 1, p.n):
                        act.wait_ge(p.pv, 4 * i)
                        need(act, p.o_tok, i - 2)
                        for side in range(2):
                            rows_ = slice(64 * side, 64 * side + 64)
                            ins = nc.scalar.activation(
                                o_raw[rows_, n, :].rearrange("p (f t) -> p f t", f=2),
                                bank[4 + n][rows_].rearrange("p (f s t) -> p f s t", f=2, s=2)[:, :, side, :], ACT.Copy)
                        ins.then_inc(p.o_raw, 1)
                    if real(i, p.n):
                        u = 4 * i + g
                        act.wait_ge(p.max, u + 1)
                        need(act, p.pT, u - 3)
                        if g == 0:
                            need(act, p.rden, i - 1)
                        for j in range(HU):
                            ins = nc.scalar.activation(probs[:, g, j, :], bank[slot(g, 2)][:, j * 128:(j + 1) * 128],
                                                       ACT.Exp, bias=neg_max[:, g, j:j + 1],
                                                       accum_out=den[:, par, HU * g + j:HU * g + j + 1])
                        ins.then_inc(p.exp, 1)

            sequences(act, p, step)

        def by_side(t, side):
            return t.rearrange("p (f s w d) -> p f s w d", f=2, s=2, d=D)[:, :, side]

        def padded(par, side, part):
            at = 64 * side + D * part
            return v_pad[:, par].rearrange("p f (w c) -> p f w c", c=WIN)[:, :, :, at:at + D]

        def attention_dve(dve, p, tail=None):
            beside = {(-1, 0): (0, 1), (0, 0): (2,), (0, 1): (3,), (0, 2): (4,), (1, 0): (5,)} if tail else {}
            if p.before:
                dve.wait_ge(*p.before)

            def step(i, par, l):
                n = 1 - par
                for g in range(UN):
                    if real(i, p.n):
                        u = 4 * i + g
                        sc = bank[slot(g, 2)][:].rearrange("p (a b) -> p a b", a=HU)
                        dve.wait_ge(p.scores, u + 1)
                        need(dve, p.exp, 4 * i + g - 3)
                        nc.vector.reduce_max(neg_max[:, g, :], sc, AX, negate=True).then_inc(p.max, 1)
                    b2, g2 = (i, g - 2) if g >= 2 else (i - 1, g + 2)
                    if real(b2, p.n):
                        u = 4 * i + g - 2
                        dve.wait_ge(p.probsT, u + 1)
                        need(dve, p.pv, u - 1)
                        nc.vector.tensor_tensor(probsT_lo[:, slot(g2, 2)].rearrange("p a b -> p (a b)"),
                                                bank[2 + slot(g2, 2)][:],
                                                probsT_hi[:, slot(g2, 2)].rearrange("p a b -> p (a b)"),
                                                ALU.subtract).then_inc(p.low, 1)
                    if g == 0 and real(i - 2, p.n):
                        dve.wait_ge(p.o_tok, i - 1)
                        parts = bank[7][:, 0:256].rearrange("p (h k d) -> p h k d", k=2, d=D)
                        heads = o_norm[:, par, :].rearrange("p (h d) -> p h d", d=D)
                        need(dve, p.o_back, i - 3)
                        nc.vector.reduce_sum(heads, parts.rearrange("p h k d -> p h d k"), AX).then_inc(p.o_norm, 1)
                        dve.wait_ge(p.o_norm, 2 * i - 3)
                        nc.vector.tensor_tensor(heads, heads, rden[:, par, :].unsqueeze(2).broadcast_to([128, H, D]),
                                                ALU.mult).then_inc(p.o_norm, 1)
                    if g == 1 and real(i - 3, p.n):
                        dve.wait_ge(p.rstd, 2 * i - 4)
                        _, b = place(p, i - 3, l)
                        nc.vector.tensor_scalar(x_all[:, bass.ts(b, C)], y[:, n, :], mv[:, n, 0:1],
                                                rs[:, n, :], ALU.subtract, ALU.mult).then_inc(p.x, 1)
                    if g == 2 and real(i - 1, p.n):
                        dve.wait_ge(p.exp, 4 * i)
                        nc.vector.reciprocal(rden[:, n, :].rearrange("p (f s m) -> p f s m", f=2, s=2),
                                             den[:, n, :].rearrange("p (f m s) -> p f s m", f=2, s=2)
                                             ).then_inc(p.rden, 1)
                    if g == 1 and real(i + 1, p.n):
                        layer, _ = place(p, i + 1, l)
                        dve.wait_ge(p.qkv, i + 2)
                        need(dve, p.scores, 4 * i)
                        nc.vector.scalar_tensor_tensor(
                            qg[:, n], bank[6][:, 0:128].unsqueeze(1).broadcast_to([128, UN, 128]), layer.bq[:, 0:1],
                            sel_q[:], ALU.add, ALU.mult)
                    if g == 2 and real(i + 1, p.n):
                        layer, _ = place(p, i + 1, l)
                        nc.vector.scalar_tensor_tensor(
                            kj[:, n], bank[6][:, 128:256].unsqueeze(1).broadcast_to([128, HU, 128]), layer.bk[:, 0:1],
                            sel_k[:], ALU.add, ALU.mult).then_inc(p.qk, 1)
                        need(dve, p.pv, 4 * i)
                        for side in range(2):
                            nc.vector.tensor_tensor(padded(n, side, 0), by_side(bank[6][:, 256:384], side),
                                                    by_side(layer.bv[:], side), ALU.add)
                        need(dve, p.v_lo, i)
                        nc.vector.tensor_tensor(v_f32[:, n, :], bank[6][:, 256:384], layer.bv[:], ALU.add).then_inc(p.v, 1)
                    if g == 3 and real(i - 2, p.n):
                        dve.wait_ge(p.proj, i - 1)
                        dve.wait_ge(p.res, i - 1)
                        nc.vector.tensor_tensor(y[:, par, :], bank[7][:, 384:512], xb[:, par, :],
                                                ALU.add).then_inc(p.y, 1)
                        dve.wait_ge(p.y, i - 1)
                        nc.vector.bn_stats(st[:, par, :], y[:, par, :])
                        dve.drain()
                        nc.vector.bn_aggr(mv[:, par, :], st[:, par, :]).then_inc(p.mv, 1)

                    if isinstance(i, int):
                        for part in beside.get((i, g), ()):
                            tail(NG - 1, part)

            sequences(dve, p, step)

        def attention_pool(pool, p, norms=None):
            if p.before:
                pool.wait_ge(*p.before)

            def step(i, par, l):
                if p is first and isinstance(i, int) and i == 0:
                    pool.wait_ge(s_w1, 16 * len(w1_act))
                if p is first and isinstance(i, int) and i == 2:
                    pool.wait_ge(s_tokens, TOKENS)
                if real(i + 2, p.n):
                    layer, b = place(p, i + 2, l)
                    if layer is not p.layers[0]:
                        pool.wait_ge(p.x, i + 3 - B)
                    need(pool, p.turned, i + 1)
                    if layer.cross:
                        nc.gpsimd.tensor_copy(cs[:, par, :], ctx_all[:, bass.ts(b, CTX)])
                    nc.gpsimd.tensor_copy(xs[:, par, :], x_all[:, bass.ts(b, C)]).then_inc(p.copied, 1)
                if p is first and real(i, p.n):
                    part = bass.ts(i, (E0 + E1) * FH // B)
                    nc.gpsimd.tensor_copy(w1_hi[:, part], w1_raw[:, part]).then_inc(s_split, 1)
                    pool.wait_ge(s_split, 2 * i + 1)
                    nc.gpsimd.tensor_tensor(w1_lo[:, part], w1_raw[:, part], w1_hi[:, part],
                                            ALU.subtract).then_inc(s_split, 1)
                if real(i + 1, p.n):
                    pool.wait_ge(p.v, i + 2)
                    for side in range(2):
                        ins = nc.gpsimd.tensor_tensor(padded(1 - par, side, 1), by_side(v_f32[:, 1 - par, :], side),
                                                      padded(1 - par, side, 0), ALU.subtract)
                    ins.then_inc(p.v_lo, 1)
                if real(i - 2, p.n):
                    need(pool, p.y, i - 3)
                    layer, b = place(p, i - 2, l)
                    nc.gpsimd.tensor_tensor(xb[:, par, :], x_all[:, bass.ts(b, C)], layer.bo[:],
                                            ALU.add).then_inc(p.res, 1)
                    pool.wait_ge(p.mv, i - 1)
                    nc.gpsimd.tensor_tensor(ve[:, par, :], mv[:, par, 1:2], ln_eps[:, 0:1],
                                            ALU.add).then_inc(p.rstd, 1)
                    pool.wait_ge(p.rstd, 2 * i - 3)
                    nc.gpsimd.tensor_tensor(rs[:, par, :], ve[:, par, :], minus_half[:, 0, 0:1],
                                            ALU.pow).then_inc(p.rstd, 1)

                if norms and isinstance(i, int) and i in (-1, 0):
                    norms(NG - 1, (i + 1,))
                if norms and isinstance(i, int) and i == 3:
                    pool.wait_ge(fusing.x, NG)

            sequences(pool, p, step)

        def cols(b):
            return slice(b * 128, (b + 1) * 128)

        def tokens(i):
            return x_all[:, bass.ts(i, GB * C)].rearrange("p (a b) -> p a b", a=GB)

        def gates_pe(pe, p):
            x, n = p.before

            def front(i):
                for h in range(2):
                    pe.wait_ge(x, n if i + h >= 2 else n - B + GB * (i + h + 1))
                    need(pe, p.vt, i + h - 1)
                    for b in range(GB):
                        nc.tensor.transpose(bank[4 * h][:, cols(b)], tokens(i + h)[:, b, :], ident[:])
                    for b in range(GB):
                        last = nc.tensor.transpose(bank[4 * h + 1][0:CTX, cols(b)],
                                                   ctx_all[:, bass.ts(GB * (i + h) + b, CTX)], ident[:])
                    last.then_inc(p.turned, 1)
                for h in range(2):
                    pe.wait_ge(p.xT, i + h + 1)
                    nc.tensor.matmul(bank[4 * h][:], wv_cos[:], xgT[:, h, :], start=True, stop=True)
                    nc.tensor.matmul(bank[4 * h + 1][:], wt_cos[:], cgT[:, h, :],
                                     start=True, stop=True).then_inc(p.proj, 1)

            def cosines(i):
                for h in range(2):
                    pe.wait_ge(p.vt, i + h + 1)
                    if i + h == 1:
                        pe.wait_ge(p.y, n)
                    need(pe, p.kept, i + h - 1)
                    need(pe, p.chain, i + h - 1)
                    for b in range(GB):
                        nc.tensor.matmul(bank[4 * h + 2][:, cols(b)], sq[:, h, cols(b)], sum_halves[:],
                                         start=True, stop=True)
                    for b in range(GB):
                        last = nc.tensor.matmul(bank[4 * h + 3][:, cols(b)], vT[:, h, cols(b)], tT[:, h, cols(b)],
                                                start=True, stop=True)
                    last.then_inc(p.cos, 1)
                for h in range(2):
                    pe.wait_ge(p.diag, i + h + 1)
                    nc.tensor.matmul(bank[4 * h + 2][:], ones[:], diag[:, h].rearrange("p a b -> p (a b)"),
                                     start=True, stop=True).then_inc(p.R, 1)

            def logits(i):
                for h in range(2):
                    if p.cosine:
                        pe.wait_ge(p.x1, i + h + 1)
                    else:
                        pe.wait_ge(x, n if i + h >= 2 else n - B + GB * (i + h + 1))
                        if i + h == 1:
                            pe.wait_ge(p.y, n)
                        need(pe, p.kept, i + h - 1)
                        need(pe, p.chain, i + h - 1)
                    for b in range(GB):
                        last = nc.tensor.transpose(bank[4 * h + 3][:, cols(b)], tokens(i + h)[:, b, :], ident[:])
                    last.then_inc(p.T1, 1)
                for h in range(2):
                    pe.wait_ge(p.x1T, i + h + 1)
                    for b in range(GB):
                        last = nc.tensor.matmul(bank[4 * h + 2][:, cols(b)], x1T[:, h, cols(b)], p.w[:],
                                                start=True, stop=True)
                    last.then_inc(p.logits, 1)

            if p.cosine:
                front(0)
                cosines(0)
                front(2)
                logits(0)
                cosines(2)
                logits(2)
            else:
                logits(0)
                logits(2)

        def gates_act(act, p):
            if p.cosine:
                act.wait_ge(s_split, 2 * B)

            def front(i):
                for h in range(2):
                    act.wait_ge(p.turned, i + h + 1)
                    nc.scalar.activation(xgT[:, h, :], bank[4 * h][:], ACT.Copy)
                    nc.scalar.activation(cgT[:, h, :], bank[4 * h + 1][0:CTX, :], ACT.Copy).then_inc(p.xT, 1)
                for h in range(2):
                    act.wait_ge(p.proj, i + h + 1)
                    need(act, p.cos, i + h - 1)
                    v, t = bank[4 * h], bank[4 * h + 1]
                    nc.scalar.activation(sq[0:XH, h, :], v[0:XH, :], ACT.Square, bias=bvx[0:XH, 0:1])
                    nc.scalar.activation(sq[XH:128, h, :], t[XH:128, :], ACT.Square, bias=btx[XH:128, 0:1])
                    nc.scalar.activation(vT[:, h, :], v[:], ACT.Identity, bias=bvx[:, 0:1])
                    nc.scalar.activation(tT[:, h, :], t[:], ACT.Identity, bias=btx[:, 0:1]).then_inc(p.vt, 1)

            def keep(i):
                for h in range(2):
                    act.wait_ge(p.T1, i + h + 1)
                    need(act, p.logits, i + h - 1)
                    need(act, p.low, i + h - 1)
                    nc.scalar.activation(x1T[:, h, :], bank[4 * h + 3][:], ACT.Copy).then_inc(p.x1T, 1)
                for h in range(2):
                    nc.scalar.activation(in_hi[:, bass.ts(i + h, GB * 128)], bank[4 * h + 3][:],
                                         ACT.Copy).then_inc(p.kept, 1)

            if p.cosine:
                front(0)
                front(2)
            keep(0)
            keep(2)
            for k in range(2):
                act.wait_ge(p.chain, NG + p.shifts * (k + 1))
                nc.scalar.activation(pr[:, pair(k), 0:p.n], hot[:, pair(k), 0:p.n], ACT.Exp).then_inc(p.exp, 1)

        def gates_dve(dve, p):
            dve.wait_ge(*p.before)
            n = p.n

            def step(i):
                if p.cosine:
                    for h in range(2):
                        dve.wait_ge(p.cos, i + h + 1)
                        nc.vector.tensor_scalar(nrm[:, h], bank[4 * h + 2][:].rearrange(
                            "p (b c) -> p b c", b=GB)[:, :, 0:2], NORM_FLOOR, None, ALU.max).then_inc(p.norms, 1)
                    for h in range(2):
                        dve.wait_ge(p.rn, i + h + 1)
                        for b in range(GB):
                            ins = nc.vector.tensor_scalar(diag[:, h, b, :], ident[:], rn[:, h, b, 1:2],
                                                          None, ALU.mult)
                        ins.then_inc(p.diag, 1)
                    for h in range(2):
                        done = 3 * (i + h)
                        dve.wait_ge(p.R, i + h + 1)
                        for b in range(GB):
                            ins = nc.vector.tensor_scalar(cosw[:, h, b, :], bank[4 * h + 2][:, cols(b)],
                                                          rn[:, h, b, 0:1], 1.0 / COS_EPS, ALU.mult, ALU.min)
                        ins.then_inc(p.sum, 1)
                        dve.wait_ge(p.sum, done + 1)
                        nc.vector.tensor_tensor(cosw[:, h], bank[4 * h + 3][:].rearrange("p (a b) -> p a b", a=GB),
                                                cosw[:, h], ALU.mult).then_inc(p.sum, 1)
                        dve.wait_ge(p.sum, done + 2)
                        nc.vector.tensor_tensor(yg[:, h], cosw[:, h], tokens(i + h), ALU.add).then_inc(p.sum, 1)
                        dve.wait_ge(p.sum, done + 3)
                        for b in range(GB):
                            nc.vector.bn_stats(gst[:, h, b, :], yg[:, h, b, :])
                        dve.drain()
                        for b in range(GB):
                            ins = nc.vector.bn_aggr(gmv[:, h, b, :], gst[:, h, b, :])
                        ins.then_inc(p.mv, 1)
                    for h in range(2):
                        dve.wait_ge(p.rstd, 2 * (i + h + 1))
                        for b in range(GB):
                            ins = nc.vector.tensor_scalar(tokens(i + h)[:, b, :], yg[:, h, b, :], gmv[:, h, b, 0:1],
                                                          grs[:, h, b:b + 1], ALU.subtract, ALU.mult)
                        ins.then_inc(p.x1, 1)
                for h in range(2):
                    dve.wait_ge(p.logits, i + h + 1)
                    nc.vector.tensor_copy(logit[:, GB * (i + h):GB * (i + h + 1), 0:n],
                                          bank[4 * h + 2][:].rearrange("p (b c) -> p b c", b=GB)[:, :, 0:n]
                                          ).then_inc(p.chain, 1)

            pairs(dve, step)
            p.links = NG
            for k in range(2):
                dve.wait_ge(p.chain, NG)
                l = logit[:, pair(k), 0:n]
                if p.b is not None:
                    link(dve, p, nc.vector.tensor_tensor(l, l, p.b[:].unsqueeze(1).broadcast_to([128, B // 2, n]),
                                                         ALU.add))
                link(dve, p, nc.vector.reduce_max(sm[:, pair(k)], l, AX))
                link(dve, p, nc.vector.tensor_tensor(hot[:, pair(k), 0:n], l,
                                                     sm[:, pair(k)].unsqueeze(2).broadcast_to([128, B // 2, n]),
                                                     ALU.subtract))
            p.chained = []
            choose(dve, p, 0)

        def pair(k):
            return slice(k * B // 2, (k + 1) * B // 2)

        def link(dve, p, ins):
            p.links += 1
            ins.then_inc(p.chain, 1)
            dve.wait_ge(p.chain, p.links)

        def choose(dve, p, k):
            n = p.n
            pn, ln, hn, c1, c2 = (t[:, pair(k), 0:n] for t in (pr, left, hot, coef1, coef2))
            m1, m2 = sm[:, pair(k)], sm2[:, pair(k)]

            def wide(t):
                return t.unsqueeze(2).broadcast_to([128, B // 2, n])

            def best(dst):
                link(dve, p, nc.vector.reduce_max(m1, ln, AX))
                link(dve, p, nc.vector.tensor_tensor(hn, ln, wide(m1), ALU.is_equal))
                link(dve, p, nc.vector.tensor_tensor(hn, hn, p.rank[:].unsqueeze(1).broadcast_to([128, B // 2, n]),
                                                     ALU.mult))
                link(dve, p, nc.vector.reduce_max(m2, hn, AX))
                link(dve, p, nc.vector.tensor_tensor(dst, hn, wide(m2), ALU.is_equal))
                link(dve, p, nc.vector.scalar_tensor_tensor(ln, dst, -2.0, ln, ALU.mult, ALU.add))

            dve.wait_ge(p.exp, k + 1)
            link(dve, p, nc.vector.reduce_sum(m1, pn, AX))
            link(dve, p, nc.vector.reciprocal(m2, m1))
            link(dve, p, nc.vector.tensor_tensor(ln, pn, wide(m2), ALU.mult))
            link(dve, p, nc.vector.tensor_copy(pn, ln))
            if p is gates0:
                best(c1)
                link(dve, p, nc.vector.tensor_copy(g1[:, pair(k)], m1))
                best(c2)
                link(dve, p, nc.vector.tensor_tensor(c2, c2, pn, ALU.mult))
            else:
                best(c1)
                best(c2)
                link(dve, p, nc.vector.tensor_tensor(c1, c1, c2, ALU.add))
                best(c2)
                link(dve, p, nc.vector.tensor_tensor(c1, c1, c2, ALU.add))
                link(dve, p, nc.vector.tensor_tensor(c1, c1, pn, ALU.mult))
                link(dve, p, nc.vector.reduce_sum(m1, c1, AX))
                link(dve, p, nc.vector.tensor_scalar(m1, m1, 1e-12, None, ALU.max))
                link(dve, p, nc.vector.reciprocal(m2, m1))
                link(dve, p, nc.vector.tensor_tensor(c1, c1, wide(m2), ALU.mult))
            p.chained.append(p.links)

        def gates_pool(pool, p):
            pool.wait_ge(*p.before)

            def step(i):
                if p.cosine:
                    for h in range(2):
                        pool.wait_ge(p.norms, i + h + 1)
                        nc.gpsimd.tensor_tensor(rn[:, h], nrm[:, h], minus_half[:], ALU.pow).then_inc(p.rn, 1)
                    for h in range(2):
                        pool.wait_ge(p.mv, i + h + 1)
                        nc.gpsimd.tensor_tensor(gve[:, h, :], gmv[:, h, :, 1], ln_eps[:], ALU.add).then_inc(p.rstd, 1)
                        pool.wait_ge(p.rstd, 2 * (i + h) + 1)
                        nc.gpsimd.tensor_tensor(grs[:, h, :], gve[:, h, :], minus_half[:, :, 0],
                                                ALU.pow).then_inc(p.rstd, 1)
                for h in range(2):
                    pool.wait_ge(p.kept, i + h + 1)
                    nc.gpsimd.tensor_tensor(in_lo[:, bass.ts(i + h, GB * 128)], x1T[:, h, :],
                                            in_hi[:, bass.ts(i + h, GB * 128)], ALU.subtract).then_inc(p.low, 1)

            pairs(pool, step)

        def experts_pe(pe, p):
            n = p.n
            pe.wait_ge(s_split, 2 * B)
            pe.wait_ge(p.gates.chain, NG)
            pe.wait_ge(p.gates.kept, NG)

            def turn_boosted(i):
                pe.wait_ge(boosting.boost, i + 1)
                for b in range(GB):
                    last = nc.tensor.transpose(bank[6][:, cols(b)], total[:, b, :], ident[:])
                last.then_inc(boosting.boostT, 1)

            def step(i):
                if p.kind == "fuse":
                    pe.wait_ge(boosting.boost_lo, i + 1)
                else:
                    pe.wait_ge(p.gates.low, i + 1)
                def up(e):
                    k = i * n + e
                    need(pe, p.h, 2 * (k - 1))
                    group = bass.ts(i, GB * 128)
                    for c in range(2):
                        at = (p.first + e) * FH + c * 128
                        dst = bank[2 * (e % 2) + c][:]
                        nc.tensor.matmul(dst, w1_hi[:, at:at + 128], in_hi[:, group], start=True, stop=False)
                        nc.tensor.matmul(dst, w1_lo[:, at:at + 128], in_hi[:, group], start=False, stop=False)
                        nc.tensor.matmul(dst, w1_hi[:, at:at + 128], in_lo[:, group],
                                         start=False, stop=True).then_inc(p.up, 1)

                def down(e):
                    k = i * n + e
                    pe.wait_ge(p.h, 2 * (k + 1))
                    need(pe, p.acc, k - 1)
                    for b in range(GB):
                        for c in range(2):
                            last = nc.tensor.matmul(bank[4 + e % 2][:, cols(b)], hid[:, e % 2, c, cols(b)],
                                                    p.w2[:, e, c, :], start=(c == 0), stop=(c == 1))
                    last.then_inc(p.down, 1)

                up(0)
                for e in range(n):
                    if e + 1 < n:
                        up(e + 1)
                    if e == 0 and p.kind == "fuse" and not real(i - 1, NG):
                        pe.wait_ge(boosting.total, NG)
                    down(e)
                    if e == 2 and p.kind == "boost" and real(i - 1, NG):
                        turn_boosted(i - 1)
                    if e == 2 and p.kind == "fuse" and not real(i - 1, NG):
                        turn_boosted(NG - 1)
                    if e == 4:
                        pe.wait_ge(p.padded, i + 1)
                        if p.kind == "boost":
                            need(pe, p.boostTs, i)
                        if p.kind == "fuse":
                            pe.wait_ge(boosting.boostTs, NG)
                        for b in range(GB):
                            last = nc.tensor.transpose(bank[6][:, cols(b)], cpad[:, b, :], ident[:])
                        last.then_inc(p.cT, 1)
                    if e == 5:
                        pe.wait_ge(p.cTs, i + 1)
                        need(pe, p.total, i)
                        for b in range(GB):
                            last = nc.tensor.matmul(bank[7][:, cols(b)], cpT[:, b, :], p.b2[:],
                                                    start=True, stop=True)
                        last.then_inc(p.b2s, 1)

            groups(pe, step)

        def experts_act(act, p):
            n = p.n

            def keep_boosted(i):
                act.wait_ge(boosting.boostT, i + 1)
                need(act, boosting.boost_lo, i)
                nc.scalar.activation(x1T[:, 0, :], bank[6][:], ACT.Copy)
                nc.scalar.activation(in_hi[:, bass.ts(i, GB * 128)], bank[6][:],
                                     ACT.Copy).then_inc(boosting.boostTs, 1)

            def step(i):
                for e in range(n):
                    k = i * n + e
                    need(act, p.down, k - 1)
                    for c in range(2):
                        act.wait_ge(p.up, 2 * k + c + 1)
                        nc.scalar.activation(hid[:, e % 2, c, :], bank[2 * (e % 2) + c][:], ACT.Relu,
                                             bias=p.b1[:, 2 * e + c:2 * e + c + 1]).then_inc(p.h, 1)
                    if e == 3 and p.kind == "boost" and real(i - 1, NG):
                        keep_boosted(i - 1)
                    if e == 3 and p.kind == "fuse" and not real(i - 1, NG):
                        keep_boosted(NG - 1)
                    if e == 5:
                        act.wait_ge(p.cT, i + 1)
                        need(act, p.b2s, i)
                        nc.scalar.activation(cpT[:].rearrange("p a b -> p (a b)"), bank[6][:],
                                             ACT.Copy).then_inc(p.cTs, 1)

            groups(act, step)

        def experts_dve(dve, p):
            n = p.n
            if p.kind == "boost":
                dve.wait_ge(p.gates.x1, NG)
            TAIL = 5 if p.kind == "fuse" else 2

            def statistics(src):
                for b in range(GB):
                    nc.vector.bn_stats(gst[:, 0, b, :], src[:, b, :])
                dve.drain()
                for b in range(GB):
                    ins = nc.vector.bn_aggr(gmv[:, 0, b, :], gst[:, 0, b, :])
                ins.then_inc(p.mv, 1)

            def normalise(dst, src, m):
                dve.wait_ge(p.rstd, 2 * m)
                for b in range(GB):
                    ins = nc.vector.tensor_scalar(dst[:, b, :], src[:, b, :], gmv[:, 0, b, 0:1],
                                                  grs[:, 0, b:b + 1], ALU.subtract, ALU.mult)
                return ins

            def every(t):
                return t[:].unsqueeze(1).broadcast_to([128, GB, C])

            def tail(i, part):
                kept = x_all[:, bass.ts(i, GB * C)].rearrange("p (a b) -> p a b", a=GB)
                if p.kind == "boost":
                    if part == 0:
                        need(dve, p.boostT, i)
                        nc.vector.scalar_tensor_tensor(
                            total[:], eo_all[:, bass.ts(i, GB * C)].rearrange("p (a b) -> p a b", a=GB), 0.5, kept,
                            ALU.mult, ALU.add).then_inc(p.boost, 1)
                    return
                if p.kind == "fuse":
                    if part == 0:
                        for b in range(GB):
                            ins = nc.vector.scalar_tensor_tensor(
                                total[:, b, :], eo_all[:, bass.ts(GB * i + b, C)], g1[:, bass.ds(GB * i + b, 1)],
                                total[:, b, :], ALU.mult, ALU.add)
                        ins.then_inc(p.tail, 1)
                        dve.wait_ge(p.tail, TAIL * i + 1)
                        nc.vector.tensor_tensor(total[:], total[:], kept, ALU.add).then_inc(p.tail, 1)
                    if part == 1:
                        dve.wait_ge(p.tail, TAIL * i + 2)
                        statistics(total)
                    if part == 2:
                        normalise(norm1, total, 2 * i + 1).then_inc(p.tail, 1)
                        dve.wait_ge(p.tail, TAIL * i + 3)
                        nc.vector.tensor_tensor(norm1[:], norm1[:], every(gamma), ALU.mult).then_inc(p.tail, 1)
                    if part == 3:
                        dve.wait_ge(p.tail, TAIL * i + 4)
                        nc.vector.tensor_tensor(norm1[:], norm1[:], every(beta), ALU.add).then_inc(p.tail, 1)
                        dve.wait_ge(p.tail, TAIL * i + 5)
                        nc.vector.tensor_tensor(total[:], norm1[:], kept, ALU.add).then_inc(p.boost, 1)
                    if part == 4:
                        dve.wait_ge(p.boost, i + 1)
                        statistics(total)
                    if part == 5:
                        normalise(kept, total, 2 * i + 2).then_inc(p.x, 1)
                    return
                if part == 0:
                    nc.vector.tensor_tensor(total[:], total[:], kept, ALU.add).then_inc(p.tail, 1)
                if part == 1:
                    dve.wait_ge(p.tail, i + 1)
                    statistics(total)
                if part == 2:
                    need(dve, p.out, 16 * i)
                    normalise(xo, total, i + 1).then_inc(p.x, 1)

            def step(i):
                for e in range(n):
                    k = i * n + e
                    dve.wait_ge(p.down, k + 1)
                    need(dve, p.acc, k)
                    for b in range(GB):
                        o = bank[4 + e % 2][:, cols(b)]
                        gate = p.coef[:].rearrange("p a b -> p (a b)")[:, bass.ds((GB * i + b) * E1 + e, 1)]
                        if e == 0:
                            ins = nc.vector.tensor_scalar(acc[:, b, :], o, gate, None, ALU.mult)
                        else:
                            ins = nc.vector.scalar_tensor_tensor(acc[:, b, :], o, gate, acc[:, b, :],
                                                                 ALU.mult, ALU.add)
                    ins.then_inc(p.acc, 1)
                    if e == 1 and p.kind != "fuse" and not real(i - 1, NG):
                        choose(dve, p.gates, 1)
                    if e < 6 and real(i - 1, NG):
                        tail(i - 1, e)
                dve.wait_ge(p.b2s, i + 1)
                dve.wait_ge(p.acc, (i + 1) * n)
                bias = bank[7][:].rearrange("p (a b) -> p a b", a=GB)
                dst = eo_all[:, bass.ts(i, GB * C)].rearrange("p (a b) -> p a b", a=GB) if p.kind == "boost" \
                    else total[:]
                if p.kind == "fuse" and not real(i - 1, NG):
                    dve.wait_ge(boosting.boostT, NG)
                if p.kind != "boost":
                    need(dve, p.x, i)
                nc.vector.tensor_tensor(dst, bias, acc[:], ALU.add).then_inc(p.total, 1)
                dve.wait_ge(p.total, i + 1)

            groups(dve, step)
            if p.kind == "fuse":
                return tail
            for part in range(6):
                tail(NG - 1, part)

        def experts_pool(pool, p):
            n = p.n
            pool.wait_ge(p.gates.chain, p.gates.chained[0])
            if p.kind == "fuse":
                pool.wait_ge(boosting.cT, NG)
            per_group = {"boost": 0, "fuse": 2, "mix": 1}[p.kind]

            def norms(i, which=range(per_group)):
                for k in which:
                    m = per_group * i + k + 1
                    pool.wait_ge(p.mv, m)
                    nc.gpsimd.tensor_tensor(gve[:, 0, :], gmv[:, 0, :, 1], ln_eps[:], ALU.add).then_inc(p.rstd, 1)
                    pool.wait_ge(p.rstd, 2 * m - 1)
                    nc.gpsimd.tensor_tensor(grs[:, 0, :], gve[:, 0, :], minus_half[:, :, 0],
                                            ALU.pow).then_inc(p.rstd, 1)

            def low_boosted(i):
                group = bass.ts(i, GB * 128)
                pool.wait_ge(boosting.boostTs, i + 1)
                nc.gpsimd.tensor_tensor(in_lo[:, group], x1T[:, 0, :], in_hi[:, group],
                                        ALU.subtract).then_inc(boosting.boost_lo, 1)

            def step(i):
                need(pool, p.cT, i)
                flat = p.coef[:].rearrange("p a b -> p (a b)")[:, bass.ts(i, GB * E1)]
                nc.gpsimd.tensor_copy(cpad[:, :, 0:n],
                                      flat.rearrange("p (a b) -> p a b", a=GB)[:, :, 0:n]).then_inc(p.padded, 1)
                if real(i - 1, NG):
                    norms(i - 1)
                    if p.kind == "boost":
                        low_boosted(i - 1)
                elif p.kind == "fuse":
                    low_boosted(NG - 1)
                else:
                    pool.wait_ge(p.gates.chain, p.gates.chained[1])

            groups(pool, step)
            if p.kind == "fuse":
                return norms
            norms(NG - 1)

        block = ctx.enter_context(nc.Block())

        @block.sync
        def _(sp):
            for dst, src in first_sp:
                sp.dma_start(dst, src).then_inc(s_first, 16)
            for dst, src in tokens_sp:
                sp.dma_start(dst, src).then_inc(s_tokens, 16)
            sp.wait_ge(s_const, 4)
            for dst, src in late_sp:
                sp.dma_start(dst, src).then_inc(s_late, 16)

            def step(i):
                sp.wait_ge(mixing.x, i + 1)
                sp.dma_start(out[bass.ts(i, GB), :, :].rearrange("b p c -> p b c"), xo[:]).then_inc(mixing.out, 16)

            groups(sp, step)
            sp.wait_ge(mixing.out, 16 * NG)

        @block.tensor
        def _(pe):
            pe.wait_ge(s_first, FIRST)
            pe.wait_ge(s_const, CONSTS)
            attention_pe(pe, first)
            pe.wait_ge(s_wT, 1)
            gates_pe(pe, gates0)
            experts_pe(pe, boosting)
            experts_pe(pe, fusing)
            attention_pe(pe, later)
            gates_pe(pe, gates1)
            experts_pe(pe, mixing)

        @block.scalar
        def _(act):
            for dst, src in first_act:
                act.dma_start(dst, src).then_inc(s_first, 16)
            for dst, src in w1_act:
                act.dma_start(dst, src).then_inc(s_w1, 16)
            attention_act(act, first)
            gates_act(act, gates0)
            experts_act(act, boosting)
            experts_act(act, fusing)
            attention_act(act, later)
            gates_act(act, gates1)
            experts_act(act, mixing)

        @block.vector
        def _(dve):
            nc.vector.memset(b2_0[:], 0.0).then_inc(s_const, 1)
            nc.vector.memset(b2_1[:], 0.0).then_inc(s_const, 1)
            nc.vector.memset(gate_w0[:], 0.0).then_inc(s_const, 1)
            nc.vector.memset(gate_w1[:], 0.0).then_inc(s_const, 1)
            nc.vector.memset(v_pad[:].rearrange("p a b c -> p (a b c)").bitcast(F32), 0.0).then_inc(s_const, 1)
            nc.vector.memset(ones[:], 1.0)
            nc.vector.memset(minus_half[:], -0.5)
            nc.vector.memset(zero_col[:], 0.0)
            nc.vector.memset(zero_row[:], 0.0)
            nc.vector.memset(cpad[:], 0.0)
            nc.vector.memset(wv_cos[:, XH:128], 0.0)
            nc.vector.memset(bvx[XH:128, :], 0.0)
            nc.vector.memset(sum_halves[:], 0.0).then_inc(s_const, 1)
            nc.vector.memset(ln_eps[:], LN_EPS).then_inc(s_const, 1)
            dve.wait_ge(s_const, 7)
            nc.vector.memset(sum_halves[0:XH, 0:1], 1.0).then_inc(s_const, 1)
            nc.vector.memset(sum_halves[XH:128, 1:2], 1.0).then_inc(s_const, 1)
            dve.wait_ge(s_first, FIRST)
            nc.vector.tensor_copy(sel_q[:], sel[:, 0, :].unsqueeze(2).broadcast_to([128, UN, 128])).then_inc(s_const, 1)
            nc.vector.tensor_copy(sel_k[:], sel[:, 1, :].unsqueeze(2).broadcast_to([128, HU, 128])).then_inc(s_const, 1)
            nc.vector.tensor_copy(ident_r[:], ident[:]).then_inc(s_const, 1)
            nc.vector.tensor_copy(causal_r[:], causal[:]).then_inc(s_const, 1)
            dve.wait_ge(s_const, CONSTS - 1)
            nc.vector.memset(sm2[:], 0.0).then_inc(s_const, 1)
            attention_dve(dve, first)
            dve.wait_ge(s_late, LATE)
            gates_dve(dve, gates0)
            experts_dve(dve, boosting)
            attention_dve(dve, later, experts_dve(dve, fusing))
            gates_dve(dve, gates1)
            experts_dve(dve, mixing)

        @block.gpsimd
        def _(pool):
            pool.wait_ge(s_first, FIRST)
            pool.wait_ge(s_const, CONSTS)
            attention_pool(pool, first)
            pool.wait_ge(s_late, LATE)
            gates_pool(pool, gates0)
            experts_pool(pool, boosting)
            attention_pool(pool, later, experts_pool(pool, fusing))
            gates_pool(pool, gates1)
            experts_pool(pool, mixing)


_INS = ['x', 'ctx_768', 'L0_attn_w_qkv', 'L0_attn_b_qkv', 'L0_attn_w_out', 'L0_attn_b_out', 'L0_xattn_Wv',
        'L0_xattn_bv', 'L0_xattn_Wt', 'L0_xattn_bt', 'L0_ffn_gate_W', 'L0_ffn_gate_b', 'L0_ffn_W1', 'L0_ffn_b1',
        'L0_ffn_W2', 'L0_ffn_b2', 'L0_ffn_ln_gamma', 'L0_ffn_ln_beta', 'L1_attn_Wq', 'L1_attn_Wk', 'L1_attn_Wv',
        'L1_attn_Wo', 'L1_xattn_wq', 'L1_xattn_bq', 'L1_xattn_wk', 'L1_xattn_bk', 'L1_xattn_wv', 'L1_xattn_bv',
        'L1_xattn_wo', 'L1_xattn_bo', 'L1_ffn_gate', 'L1_ffn_W1', 'L1_ffn_b1', 'L1_ffn_W2', 'L1_ffn_b2']


def constants():
    p = np.arange(128)
    sel = np.zeros((128, 2, UN), np.float32)
    h = p // D
    f, s, m, k = h // 8, h // 4 % 2, h // 2 % 2, h % 2
    sel[:, 0, :] = ((2 * f + m)[:, None] == np.arange(UN)) * np.float32(D ** -0.5)
    sel[:, 1, :] = (2 * k + s)[:, None] == np.arange(HU)
    return {
        "ident": np.eye(128, dtype=np.float32),
        "causal": np.where(p[:, None] >= p[None, :], 0.0, -BIG).astype(np.float32),
        "sel": sel,
        "rank0": np.arange(E0, 0, -1).astype(np.float32),
        "rank1": np.arange(E1, 0, -1).astype(np.float32),
    }


def kernel(**inputs):
    import concourse.bacc as _bacc
    from concourse.bass_utils import run_bass_kernel_spmd as _run

    nc = _bacc.Bacc("TRN2", target_bir_lowering=False, num_devices=1)
    arrays, aps = {}, {}
    given = {name: np.ascontiguousarray(inputs[name]) for name in _INS}
    for name, v in {**given, **constants()}.items():
        arrays[f"in_{name}"] = v
        aps[name] = nc.dram_tensor(f"in_{name}", v.shape, mybir.dt.from_np(v.dtype), kind="ExternalInput").ap()
    out = nc.dram_tensor("out_0", (B, T, C), F32, kind="ExternalOutput").ap()
    decoder(nc, aps, out)
    r = _run(nc, [arrays], core_ids=[0])
    return r.results[0]["out_0"]
```
